# Optimizing a Trainium2 kernel written in Bass

```python
import numpy as np
import jax
import jax.numpy as jnp

def _softmax(x, axis=-1):
    return jax.nn.softmax(x, axis=axis)

def _gelu(x):
    return jax.nn.gelu(x, approximate=True)

def _silu(x):
    return jax.nn.silu(x)

def _sigmoid(x):
    return jax.nn.sigmoid(x)

def _layernorm(x, axis=-1, eps=1e-05):
    m = jnp.mean(x, axis=axis, keepdims=True)
    v = jnp.var(x, axis=axis, keepdims=True)
    return (x - m) / jnp.sqrt(v + eps)

def _scatter_add(tgt, idx, src, axis=0):
    return tgt.at[idx].add(src)

def _segment_sum(src, seg, n):
    return jax.ops.segment_sum(src, seg, n)
kernel_name = 'mk_lm_tower_d1_tok_ids768_r4_3e7bb3'

def setup_inputs(seed: int=0):
    np.random.seed(seed)
    _w = jnp.asarray

    def _rec_inputs():
        import jax
        import jax.numpy as jnp
        _rk = jax.random.key(seed)
        x = jax.random.randint(jax.random.fold_in(_rk, 1), (64, 128), 0, 30521, jnp.int32)
        fside_BSS_adj_cooc = jax.random.uniform(jax.random.fold_in(_rk, 21), (64, 128, 128), jnp.float32, 0.0, 1)
        itok_BS_1_30519 = jax.random.randint(jax.random.fold_in(_rk, 22), (64, 128), 1, 7630, jnp.int32)
        fside_BSS_adj_het = jax.random.uniform(jax.random.fold_in(_rk, 23), (64, 128, 128), jnp.float32, 0.0, 1)
        itok_BS_0_30521 = jax.random.randint(jax.random.fold_in(_rk, 24), (64, 128), 0, 30522, jnp.int32)
        fside_BSS_adj_isg = jax.random.uniform(jax.random.fold_in(_rk, 25), (64, 128, 128), jnp.float32, 0.0, 1)
        itok_BS_1_30520 = jax.random.randint(jax.random.fold_in(_rk, 26), (64, 128), 1, 30521, jnp.int32)
        return (x, fside_BSS_adj_cooc, itok_BS_1_30519, fside_BSS_adj_het, itok_BS_0_30521, fside_BSS_adj_isg, itok_BS_1_30520)
    x, fside_BSS_adj_cooc, itok_BS_1_30519, fside_BSS_adj_het, itok_BS_0_30521, fside_BSS_adj_isg, itok_BS_1_30520 = _rec_inputs()

    def _L0_tok_setup():
        import jax, jax.numpy as jnp
        import numpy as np
        V, D = (30522, 192)
        P = 128
        B, S, G = (32, 128, 128)
        GD = 16
        LN_EPS = 1e-12

        def _vgcn(word_emb, gv_ids, adj, W, b):
            ev = word_emb[gv_ids]
            H = jnp.einsum('bgh,bhd->bgd', adj, ev)
            g = H.mean(axis=1)
            return jax.nn.relu(g @ W.T + b)
        key = jax.random.key(seed)
        ks = jax.random.split(key, 20)
        inp = {'input_ids': jax.random.randint(ks[0], (B, S), 0, V), 'adj_cooc': jax.random.uniform(ks[1], (B, G, G), jnp.float32), 'gv_cooc': jax.random.randint(ks[2], (B, G), 0, V), 'adj_het': jax.random.uniform(ks[3], (B, G, G), jnp.float32), 'gv_het': jax.random.randint(ks[4], (B, G), 0, V), 'adj_isg': jax.random.uniform(ks[5], (B, G, G), jnp.float32), 'gv_isg': jax.random.randint(ks[6], (B, G), 0, V), 'word_emb': jax.random.normal(ks[7], (V, D), jnp.float32) * 0.02, 'pos_emb': jax.random.normal(ks[8], (P, D), jnp.float32) * 0.02, 'W_cooc': jax.random.normal(ks[9], (GD, D), jnp.float32) * 0.02, 'b_cooc': jnp.zeros((GD,), jnp.float32), 'W_het': jax.random.normal(ks[10], (GD, D), jnp.float32) * 0.02, 'b_het': jnp.zeros((GD,), jnp.float32), 'W_isg': jax.random.normal(ks[11], (GD, D), jnp.float32) * 0.02, 'b_isg': jnp.zeros((GD,), jnp.float32), 'W_proj': jax.random.normal(ks[12], (D, D + 3 * GD), jnp.float32) * 0.02, 'b_proj': jnp.zeros((D,), jnp.float32), 'ln_gamma': jnp.ones((D,), jnp.float32), 'ln_beta': jnp.zeros((D,), jnp.float32)}
        return inp
    _L0_tok_all = _L0_tok_setup()
    _L0_tok_in = {k: v for k, v in _L0_tok_all.items() if k in ('word_emb', 'pos_emb', 'W_cooc', 'b_cooc', 'W_het', 'b_het', 'W_isg', 'b_isg', 'W_proj', 'b_proj', 'ln_gamma', 'ln_beta')}
    del _L0_tok_all

    def _L0_attn_setup():
        import jax, jax.numpy as jnp
        import numpy as np
        SEQ_LEN = 1024
        EMB = 3
        FILTER_ORDER = 16
        CH = 192
        BATCH = 16
        SHIFT = 0.0
        MODULATE = True
        USE_BIAS = True
        FAST_DECAY_PCT = 0.3
        SLOW_DECAY_PCT = 1.5
        TARGET = 0.01

        def _pos_emb(L):
            t = jnp.linspace(0.0, 1.0, L)
            bands = (EMB - 1) // 2
            t_rescaled = jnp.linspace(0.0, float(L - 1), L)
            w = 2.0 * jnp.pi * t_rescaled / L
            f = jnp.linspace(0.0001, float(max(bands - 1, 0)), bands)
            z_c = jnp.exp(-1j * f[None, :] * w[:, None])
            z = jnp.concatenate([t[:, None], jnp.real(z_c), jnp.imag(z_c)], axis=-1)
            return (z.astype(jnp.float32), t.astype(jnp.float32))

        def _implicit_filter(L, w1, b1, w2, b2, w3, b3, freq, deltas_abs):
            z, t = _pos_emb(L)
            h = jnp.sin(freq * (z @ w1.T + b1))
            h = jnp.sin(freq * (h @ w2.T + b2))
            h = h @ w3.T + b3
            if MODULATE:
                decay = jnp.exp(-t[:, None] * deltas_abs[None, :])
                h = h * (decay + SHIFT)
            return h

        def fft_conv(u, k):
            seqlen = u.shape[-2]
            fft_size = 2 * seqlen
            u_f = jnp.fft.rfft(u.astype(jnp.float32), n=fft_size, axis=-2)
            k_f = jnp.fft.rfft(k.astype(jnp.float32), n=fft_size, axis=-2) / fft_size
            y = jnp.fft.irfft(u_f * k_f, n=fft_size, axis=-2)[..., :seqlen, :]
            return y.astype(u.dtype)
        key = jax.random.key(seed)
        ks = jax.random.split(key, 8)
        u = jax.random.normal(ks[0], (BATCH, SEQ_LEN, CH), dtype=jnp.float32)
        w1 = jax.random.normal(ks[1], (FILTER_ORDER, EMB), dtype=jnp.float32) * 0.5
        b1 = jax.random.normal(ks[2], (FILTER_ORDER,), dtype=jnp.float32) * 0.1
        w2 = jax.random.normal(ks[3], (FILTER_ORDER, FILTER_ORDER), dtype=jnp.float32) * 0.25
        b2 = jax.random.normal(ks[4], (FILTER_ORDER,), dtype=jnp.float32) * 0.1
        w3 = jax.random.normal(ks[5], (CH, FILTER_ORDER), dtype=jnp.float32) * 0.25
        b3 = jax.random.normal(ks[6], (CH,), dtype=jnp.float32) * 0.1
        freq = jnp.ones((FILTER_ORDER,), dtype=jnp.float32)
        max_decay = np.log(TARGET) / FAST_DECAY_PCT
        min_decay = np.log(TARGET) / SLOW_DECAY_PCT
        deltas_abs = jnp.abs(jnp.linspace(min_decay, max_decay, CH)).astype(jnp.float32)
        bias = jax.random.normal(ks[7], (CH,), dtype=jnp.float32)
        return {'u': u, 'w1': w1, 'b1': b1, 'w2': w2, 'b2': b2, 'w3': w3, 'b3': b3, 'freq': freq, 'deltas_abs': deltas_abs, 'bias': bias}
    _L0_attn_all = _L0_attn_setup()
    _L0_attn_in = {k: v for k, v in _L0_attn_all.items() if k in ('w1', 'b1', 'w2', 'b2', 'w3', 'b3', 'freq', 'deltas_abs', 'bias')}
    del _L0_attn_all

    def _L0_ffn_setup():
        import jax, jax.numpy as jnp
        import numpy as np
        B, S, H, F, E, TOP_K = (4, 512, 192, 768, 8, 2)
        key = jax.random.key(seed)
        ks = jax.random.split(key, 6)
        x = jax.random.normal(ks[0], (B, S, H), dtype=jnp.float32)
        Wr = jax.random.normal(ks[1], (E, H), dtype=jnp.float32) * 0.02
        Wi = jax.random.normal(ks[2], (E, F, H), dtype=jnp.float32) * 0.02
        bi = jnp.zeros((E, F), dtype=jnp.float32)
        Wo = jax.random.normal(ks[3], (E, H, F), dtype=jnp.float32) * 0.02
        bo = jnp.zeros((E, H), dtype=jnp.float32)
        return {'x': x, 'Wr': Wr, 'Wi': Wi, 'bi': bi, 'Wo': Wo, 'bo': bo}
    _L0_ffn_all = _L0_ffn_setup()
    _L0_ffn_in = {k: v for k, v in _L0_ffn_all.items() if k in ('Wr', 'Wi', 'bi', 'Wo', 'bo')}
    del _L0_ffn_all
    return {'x': x, 'fside_BSS_adj_cooc': fside_BSS_adj_cooc, 'itok_BS_1_30519': itok_BS_1_30519, 'fside_BSS_adj_het': fside_BSS_adj_het, 'itok_BS_0_30521': itok_BS_0_30521, 'fside_BSS_adj_isg': fside_BSS_adj_isg, 'itok_BS_1_30520': itok_BS_1_30520, 'L0_tok_word_emb': _L0_tok_in['word_emb'], 'L0_tok_pos_emb': _L0_tok_in['pos_emb'], 'L0_tok_W_cooc': _L0_tok_in['W_cooc'], 'L0_tok_b_cooc': _L0_tok_in['b_cooc'], 'L0_tok_W_het': _L0_tok_in['W_het'], 'L0_tok_b_het': _L0_tok_in['b_het'], 'L0_tok_W_isg': _L0_tok_in['W_isg'], 'L0_tok_b_isg': _L0_tok_in['b_isg'], 'L0_tok_W_proj': _L0_tok_in['W_proj'], 'L0_tok_b_proj': _L0_tok_in['b_proj'], 'L0_tok_ln_gamma': _L0_tok_in['ln_gamma'], 'L0_tok_ln_beta': _L0_tok_in['ln_beta'], 'L0_attn_w1': _L0_attn_in['w1'], 'L0_attn_b1': _L0_attn_in['b1'], 'L0_attn_w2': _L0_attn_in['w2'], 'L0_attn_b2': _L0_attn_in['b2'], 'L0_attn_w3': _L0_attn_in['w3'], 'L0_attn_b3': _L0_attn_in['b3'], 'L0_attn_freq': _L0_attn_in['freq'], 'L0_attn_deltas_abs': _L0_attn_in['deltas_abs'], 'L0_attn_bias': _L0_attn_in['bias'], 'L0_ffn_Wr': _L0_ffn_in['Wr'], 'L0_ffn_Wi': _L0_ffn_in['Wi'], 'L0_ffn_bi': _L0_ffn_in['bi'], 'L0_ffn_Wo': _L0_ffn_in['Wo'], 'L0_ffn_bo': _L0_ffn_in['bo']}

def reference(x, fside_BSS_adj_cooc, itok_BS_1_30519, fside_BSS_adj_het, itok_BS_0_30521, fside_BSS_adj_isg, itok_BS_1_30520, L0_tok_word_emb, L0_tok_pos_emb, L0_tok_W_cooc, L0_tok_b_cooc, L0_tok_W_het, L0_tok_b_het, L0_tok_W_isg, L0_tok_b_isg, L0_tok_W_proj, L0_tok_b_proj, L0_tok_ln_gamma, L0_tok_ln_beta, L0_attn_w1, L0_attn_b1, L0_attn_w2, L0_attn_b2, L0_attn_w3, L0_attn_b3, L0_attn_freq, L0_attn_deltas_abs, L0_attn_bias, L0_ffn_Wr, L0_ffn_Wi, L0_ffn_bi, L0_ffn_Wo, L0_ffn_bo):
    import jax
    import jax.numpy as jnp

    def _L0_tok_ref(input_ids, adj_cooc, gv_cooc, adj_het, gv_het, adj_isg, gv_isg, word_emb, pos_emb, W_cooc, b_cooc, W_het, b_het, W_isg, b_isg, W_proj, b_proj, ln_gamma, ln_beta):
        import jax, jax.numpy as jnp
        import numpy as np
        V, D = (30522, 192)
        P = 128
        B, S, G = (32, 128, 128)
        GD = 16
        LN_EPS = 1e-12

        def _vgcn(word_emb, gv_ids, adj, W, b):
            ev = word_emb[gv_ids]
            H = jnp.einsum('bgh,bhd->bgd', adj, ev)
            g = H.mean(axis=1)
            return jax.nn.relu(g @ W.T + b)
        seq_len = input_ids.shape[1]
        emb = word_emb[input_ids] + pos_emb[:seq_len][None, :, :]
        g1 = _vgcn(word_emb, gv_cooc, adj_cooc, W_cooc, b_cooc)
        g2 = _vgcn(word_emb, gv_het, adj_het, W_het, b_het)
        g3 = _vgcn(word_emb, gv_isg, adj_isg, W_isg, b_isg)
        graph = jnp.concatenate([g1, g2, g3], axis=1)
        graph = jnp.broadcast_to(graph[:, None, :], (emb.shape[0], seq_len, graph.shape[-1]))
        x = jnp.concatenate([emb, graph], axis=2)
        y = x @ W_proj.T + b_proj
        mu = y.mean(axis=-1, keepdims=True)
        var = y.var(axis=-1, keepdims=True)
        y = (y - mu) * jax.lax.rsqrt(var + LN_EPS) * ln_gamma + ln_beta
        return y

    def _L0_attn_ref(u, w1, b1, w2, b2, w3, b3, freq, deltas_abs, bias):
        import jax, jax.numpy as jnp
        import numpy as np
        SEQ_LEN = 1024
        EMB = 3
        FILTER_ORDER = 16
        CH = 192
        BATCH = 16
        SHIFT = 0.0
        MODULATE = True
        USE_BIAS = True
        FAST_DECAY_PCT = 0.3
        SLOW_DECAY_PCT = 1.5
        TARGET = 0.01

        def _pos_emb(L):
            t = jnp.linspace(0.0, 1.0, L)
            bands = (EMB - 1) // 2
            t_rescaled = jnp.linspace(0.0, float(L - 1), L)
            w = 2.0 * jnp.pi * t_rescaled / L
            f = jnp.linspace(0.0001, float(max(bands - 1, 0)), bands)
            z_c = jnp.exp(-1j * f[None, :] * w[:, None])
            z = jnp.concatenate([t[:, None], jnp.real(z_c), jnp.imag(z_c)], axis=-1)
            return (z.astype(jnp.float32), t.astype(jnp.float32))

        def _implicit_filter(L, w1, b1, w2, b2, w3, b3, freq, deltas_abs):
            z, t = _pos_emb(L)
            h = jnp.sin(freq * (z @ w1.T + b1))
            h = jnp.sin(freq * (h @ w2.T + b2))
            h = h @ w3.T + b3
            if MODULATE:
                decay = jnp.exp(-t[:, None] * deltas_abs[None, :])
                h = h * (decay + SHIFT)
            return h

        def fft_conv(u, k):
            seqlen = u.shape[-2]
            fft_size = 2 * seqlen
            u_f = jnp.fft.rfft(u.astype(jnp.float32), n=fft_size, axis=-2)
            k_f = jnp.fft.rfft(k.astype(jnp.float32), n=fft_size, axis=-2) / fft_size
            y = jnp.fft.irfft(u_f * k_f, n=fft_size, axis=-2)[..., :seqlen, :]
            return y.astype(u.dtype)
        L = u.shape[-2]
        k = _implicit_filter(L, w1, b1, w2, b2, w3, b3, freq, deltas_abs)
        y = fft_conv(u, k)
        if USE_BIAS:
            y = y + u * bias
        return y

    def _L0_ffn_ref(x, Wr, Wi, bi, Wo, bo):
        import jax, jax.numpy as jnp
        import numpy as np
        B, S, H, F, E, TOP_K = (4, 512, 192, 768, 8, 2)
        xf = x.reshape(-1, x.shape[-1])
        router_logits = jnp.einsum('th,eh->te', xf, Wr)
        topk_vals, topk_idx = jax.lax.top_k(router_logits, TOP_K)
        routing_weights = jax.nn.softmax(topk_vals, axis=-1)
        h = jnp.einsum('th,efh->etf', xf, Wi) + bi[:, None, :]
        h = jax.nn.gelu(h, approximate=False)
        expert_out = jnp.einsum('etf,ehf->eth', h, Wo) + bo[:, None, :]
        expert_out = jnp.transpose(expert_out, (1, 0, 2))
        gathered = jnp.take_along_axis(expert_out, topk_idx[:, :, None], axis=1)
        out = jnp.einsum('tk,tkh->th', routing_weights, gathered)
        return out.reshape(x.shape)
    h = _L0_tok_ref(x, fside_BSS_adj_cooc, itok_BS_1_30519, fside_BSS_adj_het, itok_BS_0_30521, fside_BSS_adj_isg, itok_BS_1_30520, L0_tok_word_emb, L0_tok_pos_emb, L0_tok_W_cooc, L0_tok_b_cooc, L0_tok_W_het, L0_tok_b_het, L0_tok_W_isg, L0_tok_b_isg, L0_tok_W_proj, L0_tok_b_proj, L0_tok_ln_gamma, L0_tok_ln_beta)
    h = h + _L0_attn_ref(_layernorm(h, axis=-1), L0_attn_w1, L0_attn_b1, L0_attn_w2, L0_attn_b2, L0_attn_w3, L0_attn_b3, L0_attn_freq, L0_attn_deltas_abs, L0_attn_bias)
    h = h + _L0_ffn_ref(_layernorm(h, axis=-1), L0_ffn_Wr, L0_ffn_Wi, L0_ffn_bi, L0_ffn_Wo, L0_ffn_bo)
    return h

_drawn_inputs = setup_inputs


def setup_inputs(seed=0):
    import zlib

    import numpy as np

    out = dict(_drawn_inputs(seed))
    spreads = {'L0_tok_b_cooc': (0.0, 0.1),
     'L0_tok_b_het': (0.0, 0.1),
     'L0_tok_b_isg': (0.0, 0.1),
     'L0_tok_b_proj': (0.0, 0.1),
     'L0_tok_ln_gamma': (1.0, 0.2),
     'L0_tok_ln_beta': (0.0, 0.1),
     'L0_attn_freq': (1.0, 0.6),
     'L0_ffn_bi': (0.0, 0.6),
     'L0_ffn_bo': (0.0, 0.1)}
    factors = {'fside_BSS_adj_cooc': 8.0,
     'fside_BSS_adj_het': 8.0,
     'fside_BSS_adj_isg': 8.0,
     'L0_tok_W_cooc': 3.617,
     'L0_tok_W_het': 2.735,
     'L0_tok_W_isg': 3.347,
     'L0_attn_w1': 43.194,
     'L0_attn_b1': 125.26,
     'L0_attn_b2': 50.507,
     'L0_attn_w3': 17.268,
     'L0_attn_b3': 117.054,
     'L0_attn_deltas_abs': 175.706,
     'L0_attn_w2': 15.252}
    for name, (base, spread) in spreads.items():
        noise = np.random.default_rng([zlib.crc32(name.encode()), seed]).standard_normal(out[name].shape)
        drawn = base * np.exp(spread * noise) if base else spread * noise
        out[name] = jnp.asarray(drawn.astype(out[name].dtype))
    for name, factor in factors.items():
        out[name] = (out[name] * factor).astype(out[name].dtype)
    return out
```

```python
from contextlib import ExitStack

import concourse.bass as bass
from concourse import mybir

B, S, D = 64, 128, 192
V = 30522
GRAPHS, GD = 3, 16
E, F = 8, 768
D0 = 128
D1 = D - D0
PG = D1 + GRAPHS * GD
Q = 4
NQ = B // Q
FC = F // 128
WE = 2 * F + FC * D
BLOB = WE + FC + D
XROW = 2 * D + 4
TS = 256
NT = 2 * B * S // TS + E
NC = NT * TS // 128
CC = 8
NCH = D // CC
RING = 4
NFFT = 2 * S
EPS_TOK, EPS_LN = 1e-12, 1e-5
TWO_PI = 6.283185307179586
C1 = 6.28125
C2 = 0.0019350051879882812
C3 = TWO_PI - C1 - C2
MAGIC = 12582912.0
SPARE = TS


def tower(nc, t, out):
    fp32, bf16, i32, u32 = mybir.dt.float32, mybir.dt.bfloat16, mybir.dt.int32, mybir.dt.uint32
    ALU, ACT, AX = mybir.AluOpType, mybir.ActivationFunctionType, mybir.AxisListType
    ctx = ExitStack()
    with ctx:
        def sb(name, shape, dt=fp32):
            return ctx.enter_context(nc.sbuf_tensor(name, shape, dt))

        def sem(name):
            return ctx.enter_context(nc.semaphore(name))

        def repeat(ap, at, n):
            dims = [list(d) for d in ap.ap]
            dims.insert(at, [0, n])
            return bass.AP(tensor=ap.tensor, offset=ap.offset, ap=dims)

        def reverse(ap):
            dims = [list(d) for d in ap.ap]
            step, n = dims[-1]
            dims[-1] = [-step, n]
            return bass.AP(tensor=ap.tensor, offset=ap.offset + step * (n - 1), ap=dims)

        def after(eng, semaphore, value):
            if not isinstance(value, int) or value > 0:
                eng.wait_ge(semaphore, value)

        def steps(eng, n, body, first=1, last=0):
            for it in range(first):
                body(it)
            with eng.Fori(first, n - last) as it:
                body(it)
            for it in range(n - last, n):
                body(it)

        out_rows = out[0:B * S, :].rearrange("(b s) d -> b s d", s=S)

        kpad_d = nc.dram_tensor("kpad_d", (D, NFFT), fp32).ap()
        xtab_d = nc.dram_tensor("xtab_d", (B * S, XROW // 2), fp32).ap()
        blob_d = nc.dram_tensor("blob_d", (E, 128, BLOB), fp32).ap()

        ident = sb("ident", [128, 128])
        identb = sb("identb", [128, 128], bf16)
        tri = sb("tri", [128, 128], bf16)
        ones_b = sb("ones_b", [128, 128], bf16)
        zero_f = sb("zero_f", [128, 2, D])
        zero_b = zero_f[:, 0, :].bitcast(bf16)
        iota_f = sb("iota_f", [128, 256])
        iota_b = sb("iota_b", [128, 256], bf16)
        cst = sb("cst", [128, 128 + 128 + 256 + 128 + 1 + NC])
        mean_w = sb("mean_w", [128, 1])
        ids_i = sb("ids_i", [128, 1 + GRAPHS, B], i32)
        idx = sb("idx", [128, 2, Q * (1 + GRAPHS)], i32)
        wp0 = sb("wp0", [128, D])
        wp1 = sb("wp1", [PG, D])
        pos = sb("pos", [128, D])
        posb = sb("posb", [128, D])
        posT0 = sb("posT0", [128, 128])
        posT1 = sb("posT1", [D1, 128])
        bproj = sb("bproj", [128, D])
        gamma = sb("gamma", [128, D])
        beta = sb("beta", [128, D])
        wg = sb("wg", [128, 2, GRAPHS, GRAPHS * GD])
        gbias = sb("gbias", [128, 1])
        wr = sb("wr", [128, 2, E])
        filt = sb("filt", [128, 2, 4])
        small = sb("small", [16, 3 + 16 + 16 + D + 128])
        kT = sb("kT", [128, 2, NFFT])
        dec = sb("dec", [128, 2, 128])
        sinb = sb("sinb", [16, 5, 128])

        emb_g = sb("emb_g", [128, 2, Q, D])
        ev_g = sb("ev_g", [128, 2, GRAPHS, Q, D])
        adj_s = sb("adj_s", [128, 2, GRAPHS, Q, 128])
        col_s = sb("col_s", [128, GRAPHS * Q])
        gt_s = sb("gt_s", [128, 2, GRAPHS * Q])
        xt0 = sb("xt0", [128, Q * 128])
        xt1 = sb("xt1", [128, Q * 128])
        ys = sb("ys", [128, Q, D])
        stats = sb("stats", [128, Q, 6])
        mv = sb("mv", [128, Q, 2])
        rs = sb("rs", [128, 4, Q])

        Hs = sb("Hs", [128, B, D])
        U = sb("U", [128, D * B])
        Ut = U[:, :].rearrange("p (c b) -> p c b", b=B)
        toep = sb("toep", [128, RING, CC, 128])

        wst = sb("wst", [128, WE])
        blob = sb("blob", [128, BLOB])

        xn = emb_g
        old_adj = adj_s[:, :, :, :, :].rearrange("p a j q h -> p (a j q h)")
        xrow_f = old_adj[:, 0:Q * XROW].rearrange("p (a q x) -> p a q x", a=2, q=Q)
        xrow = old_adj[:, 0:Q * XROW].bitcast(bf16).rearrange("p (a q x) -> p a q x", a=2, q=Q)
        xnT0 = old_adj[:, 1664:1664 + Q * 128]
        xnT1 = old_adj[0:D1, 2176:2176 + Q * 128]
        lg = sb("lg", [128, Q, E])
        top = sb("top", [128, Q, E])
        topi = sb("topi", [128, Q, E], u32)
        wsm = sb("wsm", [128, 4, Q])
        e01 = sb("e01", [128, 2, B])

        rt = ev_g[:, :, :, :, :].rearrange("p a g q d -> p (a g q d)")
        at = [0]

        def carve(n):
            at[0] += n
            assert at[0] <= 2 * GRAPHS * Q * D
            return rt[:, at[0] - n:at[0]]

        oh = [carve(E * B).rearrange("p (e b) -> p e b", e=E) for _ in range(2)]
        sl = carve(E * B).rearrange("p (e b) -> p e b", e=E)
        run = carve(E * B).rearrange("p (e b) -> p e b", e=E)
        onesf = carve(B)
        ohb = sb("ohb", [128, E, B], bf16)
        cnt = carve(4 * E).rearrange("p (a e) -> p a e", a=4)
        slot = carve(2 * B).rearrange("p (k b) -> p k b", k=2)
        slq = carve(2 * B).rearrange("p (k b) -> p k b", k=2)
        slp = carve(2 * B).rearrange("p (k b) -> p k b", k=2)
        sloti = sb("sloti", [128, 3, 2, B], i32)
        cnti = sb("cnti", [128, 2, E], i32)
        tv = carve(2)
        row_t = carve(NC)
        row_k = sb("row_k", [128, NC])
        row_o = carve(NC)
        id_f = carve(NC)
        id_g = sb("id_g", [128, NC], i32)
        id_s = sb("id_s", [128, NC], i32)
        eidf = carve(NT * E).rearrange("p (t e) -> p t e", e=E)
        eidr = carve(NT)
        eid = sb("eid", [1, NT], i32)
        tp = wst[:, 0:2 * CC * 128].rearrange("p (a c t) -> p a c t", a=2, c=CC)
        pick = wst[:, 0:1536].bitcast(bf16).rearrange("p (r a n) -> p r a n", r=4, a=3)

        at_u = [0]

        def carve_u(n):
            at_u[0] += n
            assert at_u[0] <= D * B
            return U[:, at_u[0] - n:at_u[0]]

        wbuf = [carve_u(BLOB) for _ in range(2)]
        hf = [carve_u(FC * TS).rearrange("p (f n) -> p f n", f=FC) for _ in range(2)]
        hh = [carve_u(FC * TS // 2).bitcast(bf16).rearrange("p (f n) -> p f n", f=FC) for _ in range(2)]
        hl = [carve_u(FC * TS // 2).bitcast(bf16).rearrange("p (f n) -> p f n", f=FC) for _ in range(2)]
        xg_f = blob[:, 0:2 * XROW].rearrange("p (a h x) -> p a h x", a=2, h=2)
        xg = blob[:, 0:2 * XROW].bitcast(bf16).rearrange("p (a h x) -> p a h x", a=2, h=2)
        xgT = blob[:, 800:800 + 3 * TS].bitcast(bf16).rearrange("p (a c n) -> p a c n", a=2, c=3)
        yo = blob[:, 1600:1600 + 4 * D].rearrange("p (a h d) -> p a h d", a=2, h=2)
        gi = sb("gi", [128, 2, 2], i32)
        si = sb("si", [128, 2, 2], i32)
        wk = sb("wk", [128, 2, 2, 2])

        bank = [ctx.enter_context(nc.psum_tensor(f"bank{i}", [128, 512], fp32)) for i in range(8)]

        loaded = sem("loaded")
        cast_done = sem("cast_done")
        filt_step = sem("filt_step")
        filt_in = sem("filt_in")
        filt_arg = sem("filt_arg")
        kpad_stored = sem("kpad_stored")
        kready = sem("kready")
        dec_done = sem("dec_done")
        pos_done = sem("pos_done")
        pos_t = sem("pos_t")
        pos_ts = sem("pos_ts")
        adj_in = [sem(f"adj_in{p}") for p in range(2)]
        idx_staged = sem("idx_staged")
        emb_in = [sem(f"emb_in{p}") for p in range(2)]
        ev_in = [sem(f"ev_in{p}") for p in range(2)]
        pool_turn = sem("pool_turn")
        colsum = sem("colsum")
        col_ready = sem("col_ready")
        emb_t = sem("emb_t")
        xt_ready = sem("xt_ready")
        gvec = sem("gvec")
        gvec_ready = sem("gvec_ready")
        gfeat = sem("gfeat")
        gfeat_ready = sem("gfeat_ready")
        proj = sem("proj")
        proj_read = sem("proj_read")
        rows_done = sem("rows_done")
        w_in = sem("w_in")
        w_hi = sem("w_hi")
        w_lo = sem("w_lo")
        w_out = sem("w_out")
        toep_in = [sem(f"toep_in{s}") for s in range(RING)]
        turned = sem("turned")
        conv = sem("conv")
        conv_read = sem("conv_read")
        ln_done = sem("ln_done")
        hi_done = sem("hi_done")
        lo_done = sem("lo_done")
        xrow_out = [sem(f"xrow_out{p}") for p in range(2)]
        h_out = sem("h_out")
        xn_t = sem("xn_t")
        xnT_ready = sem("xnT_ready")
        logits = sem("logits")
        gap_ready = sem("gap_ready")
        exp_done = sem("exp_done")
        wts_done = sem("wts_done")
        hot_ready = sem("hot_ready")
        ranks = sem("ranks")
        pick_ready = sem("pick_ready")
        pick_used = sem("pick_used")
        table = sem("table")
        ids_done = sem("ids_done")
        wb_in = [sem(f"wb_in{p}") for p in range(2)]
        stage_done = sem("stage_done")
        xg_in = [sem(f"xg_in{p}") for p in range(2)]
        xg_t = sem("xg_t")
        xgT_ready = sem("xgT_ready")
        up = sem("up")
        gelu = sem("gelu")
        hid = sem("hid")
        down = sem("down")
        biased = sem("biased")
        yo_ready = sem("yo_ready")
        scat = [sem(f"scat{h}") for h in range(2)]

        block = ctx.enter_context(nc.Block())

        N_LOADS = 28

        @block.sync
        def _(sp):
            n = [0]

            def load(dst, src):
                n[0] += 1
                sp.dma_start(dst, src).then_inc(loaded, 16)

            load(ids_i[:, :, :], t["ids"].rearrange("p (j b) -> p j b", j=1 + GRAPHS))
            load(cst[:, :], t["cst"])
            load(wp0[:, :], t["WpT"][0:D0, :])
            load(wp1[:, :], t["WpT"][D0:D0 + PG, :])
            load(pos[:, :], t["pos"])
            load(bproj[:, :], t["b_proj"].partition_broadcast(128))
            load(gamma[:, :], t["gamma"].partition_broadcast(128))
            load(beta[:, :], t["beta"].partition_broadcast(128))
            for j in range(GRAPHS):
                load(wg[:, 0, j, j * GD:(j + 1) * GD], t["WgT"][0:D0, j * GD:(j + 1) * GD])
                load(wg[0:D1, 1, j, j * GD:(j + 1) * GD], t["WgT"][D0:D, j * GD:(j + 1) * GD])
            load(gbias[D1:PG, :], t["gbias"])
            load(wr[:, 0, :], t["WrT"][0:D0, :])
            load(wr[0:D1, 1, :], t["WrT"][D0:D, :])
            for i, name in enumerate(("deltas", "b3", "bias")):
                load(filt[:, 0, i:i + 1], t[name][0:D0, :])
                load(filt[0:D1, 1, i:i + 1], t[name][D0:D, :])
            load(small[0:3, 0:16], t["w1T"])
            load(small[:, 16:32], t["w2T"])
            load(small[:, 32:32 + D], t["w3T"])
            load(small[:, 32 + D:32 + D + 3], t["cols"])
            load(small[0:3, 35 + D:35 + D + 128], t["zT"])
            assert n[0] == N_LOADS, n[0]

            def load_adj(i, p):
                for j in range(GRAPHS):
                    sp.dma_start(adj_s[:, p, j, :, :],
                                 t["adj"][j][bass.ds(i * Q, Q), :, :].rearrange("b g h -> g b h")).then_inc(adj_in[p], 16)

            load_adj(0, 0)
            load_adj(1, 1)
            with sp.Fori(0, NQ // 2 - 1) as it:
                for p in range(2):
                    sp.wait_ge(colsum, 2 * it + p + 1)
                    load_adj(2 * it + p + 2, p)

            sp.wait_ge(kready, 2)
            sp.dma_start(kpad_d[0:D0, :], kT[:, 0, :]).then_inc(kpad_stored, 16)
            sp.dma_start(kpad_d[D0:D, :], kT[0:D1, 1, :]).then_inc(kpad_stored, 16)
            sp.wait_ge(kpad_stored, 32)

            def load_toep(c, s):
                src = bass.AP(tensor=kpad_d.tensor, offset=c * (CC * NFFT), ap=[[1, 128], [NFFT, CC], [1, 128]])
                sp.dma_start(toep[:, s, :, :], src).then_inc(toep_in[s], 16)

            for s in range(RING):
                load_toep(s, s)
            with sp.Fori(1, NCH // RING) as it:
                for s in range(RING):
                    sp.wait_ge(turned, it * RING + s + 1 - RING)
                    load_toep(it * RING + s, s)

            def store_rows(i, p):
                sp.dma_start(out_rows[bass.ds(i * Q, Q), :, :].rearrange("b s d -> s b d"),
                             Hs[:, bass.ds(i * Q, Q), :]).then_inc(h_out, 16)
                sp.wait_ge(wts_done, i + 1)
                sp.dma_start(xtab_d[bass.ds(i * (Q * S), Q * S), :].rearrange("(b s) x -> s b x", s=S),
                             xrow_f[:, p, :, :]).then_inc(xrow_out[p], 16)

            sp.wait_ge(cast_done, 1)
            sp.dma_start(out[B * S:B * S + SPARE, :].rearrange("(a p) d -> p a d", a=2),
                         zero_f[:, :, :]).then_inc(h_out, 16)
            sp.wait_ge(conv_read, NCH)
            with sp.Fori(0, NQ // 2) as it:
                for p in range(2):
                    store_rows(2 * it + p, p)

            sp.wait_ge(w_out, 16 * E)
            sp.wait_ge(ids_done, 1)

            def load_w(q, p):
                e = sp.value_load(eid[0:1, bass.ds(q, 1)], min_val=0, max_val=E - 1)
                sp.dma_start(wbuf[p], blob_d[bass.ds(e, 1), :, :].rearrange("e p x -> p (e x)")).then_inc(wb_in[p], 16)

            load_w(0, 0)
            load_w(1, 1)
            with sp.Fori(1, NT // 2) as it:
                for p in range(2):
                    sp.wait_ge(biased, 2 * it + p - 1)
                    load_w(2 * it + p, p)
            sp.wait_ge(h_out, 16 * (NQ + 1))
            for p in range(2):
                sp.wait_ge(scat[p], 16 * NT)

        @block.gpsimd
        def _(pool):
            def gathers(i, p):
                pool.wait_ge(idx_staged, i + 1)
                pool.sem_inc(pool_turn, 1)
                for b in range(Q):
                    pool.indirect_dma_start(emb_g[:, p, b, :], None, t["word_emb"],
                                            bass.IndirectOffsetOnAxis(ap=idx[:, p, b:b + 1], axis=0)).then_inc(emb_in[p], 16)
                for j in range(GRAPHS):
                    for b in range(Q):
                        k = (1 + j) * Q + b
                        pool.indirect_dma_start(ev_g[:, p, j, b, :], None, t["word_emb"],
                                                bass.IndirectOffsetOnAxis(ap=idx[:, p, k:k + 1], axis=0)).then_inc(ev_in[p], 16)

            gathers(0, 0)
            gathers(1, 1)
            with pool.Fori(1, NQ // 2) as it:
                for p in range(2):
                    pool.wait_ge(gvec, 2 * it + p - 1)
                    pool.sem_inc(pool_turn, 1)
                    gathers(2 * it + p, p)

            def fetch(q, p):
                pool.wait_ge(stage_done, q + 1)
                pool.sem_inc(pool_turn, 1)
                for h in range(2):
                    pool.indirect_dma_start(xg_f[:, p, h, :], None, xtab_d,
                                            bass.IndirectOffsetOnAxis(ap=gi[:, p, h:h + 1], axis=0)).then_inc(xg_in[p], 16)

            def add_rows(q, p):
                for h in range(2):
                    after(pool, scat[h], 16 * q)
                pool.wait_ge(yo_ready, q + 1)
                pool.sem_inc(pool_turn, 1)
                for h in range(2):
                    pool.indirect_dma_start(out, bass.IndirectOffsetOnAxis(ap=si[:, p, h:h + 1], axis=0), yo[:, p, h, :], None,
                                            compute_op=ALU.add).then_inc(scat[h], 16)

            for p in range(2):
                pool.wait_ge(xrow_out[p], 16 * (NQ // 2))
            pool.wait_ge(h_out, 16 * (NQ + 1))
            fetch(0, 0)
            fetch(1, 1)

            def tiles(it):
                for p in range(2):
                    q = 2 * it + p
                    if not (isinstance(q, int) and q + 2 >= NT):
                        fetch(q + 2, p)
                    if not (isinstance(q, int) and q < 2):
                        add_rows(q - 2, p)

            steps(pool, NT // 2, tiles, first=2, last=1)
            for p in range(2):
                add_rows(NT - 2 + p, p)

        @block.tensor
        def _(pe):
            mm = nc.tensor.matmul
            pe.wait_ge(loaded, 16 * N_LOADS)
            z = small[0:3, 35 + D:35 + D + 128]
            mm(bank[0][0:16, 0:128], small[0:3, 0:16], z, start=True, stop=True).then_inc(filt_step, 1)
            nc.tensor.transpose(bank[1][:, 0:128], pos[:, 0:D0], cst[:, 0:128])
            nc.tensor.transpose(bank[1][0:D1, 128:256], pos[:, D0:D], cst[:, 0:128]).then_inc(pos_t, 1)
            pe.wait_ge(pos_ts, 1)
            mm(bank[2][:, 0:D], posT0[:, :], wp0[:, :], start=True, stop=False)
            mm(bank[2][:, 0:D], posT1[:, :], wp1[0:D1, :], start=False, stop=True).then_inc(pos_t, 1)
            pe.wait_ge(filt_in, 1)
            mm(bank[0][0:16, 128:256], small[:, 16:32], sinb[:, 3, :], start=True, stop=True).then_inc(filt_step, 1)
            pe.wait_ge(filt_in, 2)
            mm(bank[0][:, 256:384], small[:, 32:32 + D0], sinb[:, 4, :], start=True, stop=True)
            mm(bank[0][0:D1, 384:512], small[:, 32 + D0:32 + D], sinb[:, 4, :], start=True, stop=True).then_inc(filt_step, 1)
            pe.wait_ge(kready, 2)
            pe.wait_ge(pos_done, 1)
            pe.wait_ge(cast_done, 1)

            def quad(it, p):
                i = 2 * it + p
                pe.wait_ge(adj_in[p], 16 * GRAPHS * (it + 1))
                for j in range(GRAPHS):
                    for b in range(Q):
                        k = j * Q + b
                        last = mm(bank[0][:, k:k + 1], adj_s[:, p, j, b, :], mean_w[:, :], start=True, stop=True)
                last.then_inc(colsum, 1)
                pe.wait_ge(emb_in[p], 16 * Q * (it + 1))
                for b in range(Q):
                    nc.tensor.transpose(bank[1][:, b * 128:(b + 1) * 128], emb_g[:, p, b, 0:D0], ident[:, :])
                    last = nc.tensor.transpose(bank[2][0:D1, b * 128:(b + 1) * 128], emb_g[:, p, b, D0:D], ident[:, :])
                last.then_inc(emb_t, 1)
                pe.wait_ge(col_ready, i + 1)
                pe.wait_ge(ev_in[p], 16 * GRAPHS * Q * (it + 1))
                for j in range(GRAPHS):
                    for b in range(Q):
                        k = j * Q + b
                        mm(bank[0][:, 64 + k:65 + k], ev_g[:, p, j, b, 0:D0], col_s[:, k:k + 1], start=True, stop=True)
                        last = mm(bank[0][0:D1, 80 + k:81 + k], ev_g[:, p, j, b, D0:D], col_s[:, k:k + 1], start=True, stop=True)
                last.then_inc(gvec, 1)
                pe.wait_ge(gvec_ready, i + 1)
                for j in range(GRAPHS):
                    mm(bank[3][D1:PG, 0:Q], wg[:, 0, j, :], gt_s[:, 0, j * Q:(j + 1) * Q], start=j == 0, stop=False)
                    last = mm(bank[3][D1:PG, 0:Q], wg[0:D1, 1, j, :], gt_s[0:D1, 1, j * Q:(j + 1) * Q], start=False, stop=j == GRAPHS - 1)
                last.then_inc(gfeat, 1)
                pe.wait_ge(xt_ready, i + 1)
                pe.wait_ge(gfeat_ready, i + 1)
                for b in range(Q):
                    ps = bank[4 + b // 2][:, (b % 2) * D:(b % 2 + 1) * D]
                    mm(ps, xt0[:, b * 128:(b + 1) * 128], wp0[:, :], start=True, stop=False)
                    last = mm(ps, xt1[0:PG, b * 128:(b + 1) * 128], wp1[:, :], start=False, stop=True)
                last.then_inc(proj, 1)

            quad(0, 0)
            pe.wait_ge(proj_read, 1)
            quad(0, 1)
            with pe.Fori(1, NQ // 2) as it:
                for p in range(2):
                    pe.wait_ge(proj_read, 2 * it + p)
                    quad(it, p)

            pe.wait_ge(rows_done, NQ)

            def chunk(it, s):
                c = it * RING + s
                pe.wait_ge(turned, c + 1)
                for k in range(CC):
                    last = mm(bank[6 + s % 2][:, k * B:(k + 1) * B], tp[:, s % 2, k, :],
                              Ut[:, bass.ds(c * CC + k, 1), :].rearrange("p c b -> p (c b)"), start=True, stop=True)
                last.then_inc(conv, 1)

            for s in range(RING):
                if s >= 2:
                    pe.wait_ge(conv_read, s - 1)
                chunk(0, s)
            with pe.Fori(1, NCH // RING) as it:
                for s in range(RING):
                    pe.wait_ge(conv_read, it * RING + s - 1)
                    chunk(it, s)

            def route(it, p):
                i = 2 * it + p
                pe.wait_ge(ln_done, i + 1)
                for b in range(Q):
                    nc.tensor.transpose(bank[1][:, b * 128:(b + 1) * 128], xn[:, p, b, 0:D0], ident[:, :])
                    last = nc.tensor.transpose(bank[2][0:D1, b * 128:(b + 1) * 128], xn[:, p, b, D0:D], ident[:, :])
                last.then_inc(xn_t, 1)
                pe.wait_ge(xnT_ready, i + 1)
                for b in range(Q):
                    ps = bank[3][:, b * E:(b + 1) * E]
                    mm(ps, xnT0[:, b * 128:(b + 1) * 128], wr[:, 0, :], start=True, stop=False)
                    last = mm(ps, xnT1[:, b * 128:(b + 1) * 128], wr[0:D1, 1, :], start=False, stop=True)
                last.then_inc(logits, 1)

            with pe.Fori(0, NQ // 2) as it:
                for p in range(2):
                    route(it, p)

            pe.wait_ge(hot_ready, 1)
            hot = ohb[:, :, :].rearrange("p e b -> p (e b)")
            mm(bank[4][:, :], tri[:, :], hot, start=True, stop=True)
            mm(bank[5][:, :], ones_b[:, :], hot, start=True, stop=True).then_inc(ranks, 1)

            mm(bank[6][:, 0:NC], zero_b[:, 0:128], zero_b[:, 0:NC], start=True, stop=False)
            mm(bank[7][:, 0:NC], zero_b[:, 0:128], zero_b[:, 0:NC], start=True, stop=False)
            with pe.Fori(0, B // 2) as it:
                for r in range(4):
                    pe.wait_ge(pick_ready, 4 * it + r + 1)
                    mm(bank[6][:, 0:NC], pick[:, r, 0, 0:128], pick[:, r, 2, 0:NC], start=False, stop=False)
                    mm(bank[7][:, 0:NC], pick[:, r, 1, 0:128], pick[:, r, 2, 0:NC], start=False, stop=False).then_inc(pick_used, 1)
            mm(bank[6][:, 0:NC], zero_b[:, 0:128], zero_b[:, 0:NC], start=False, stop=True)
            mm(bank[7][:, 0:NC], zero_b[:, 0:128], zero_b[:, 0:NC], start=False, stop=True).then_inc(table, 1)
            pe.wait_ge(ids_done, 1)

            xT_ps = bank[0][:, :].bitcast(bf16)

            def views(p):
                w = wbuf[p]
                hi = w[:, 0:WE // 2].bitcast(bf16)
                lo = w[:, WE // 2:WE].bitcast(bf16)
                return hi, lo

            def turn_rows(it, p):
                pe.wait_ge(xg_in[p], 32 * (it + 1))
                for h in range(2):
                    for c in range(3):
                        last = nc.tensor.transpose(xT_ps[:, c * TS + h * 128:c * TS + h * 128 + 128],
                                                   xg[:, p, h, c * 128:(c + 1) * 128], identb[:, :])
                last.then_inc(xg_t, 1)

            def up_tile(it, p):
                q = 2 * it + p
                hi, lo = views(p)
                pe.wait_ge(xgT_ready, q + 1)
                pe.wait_ge(wb_in[p], 16 * (it + 1))
                after(pe, gelu, FC * q)
                x0, x1, x2 = (xgT[:, p, c, :] for c in range(3))
                for f in range(FC):
                    ps = bank[2 + f // 2][:, (f % 2) * TS:(f % 2 + 1) * TS]
                    a = slice(f * 128, (f + 1) * 128)
                    r = slice(F + f * 128, F + (f + 1) * 128)
                    mm(ps, hi[:, a], x0, start=True, stop=False)
                    mm(ps, hi[:, a], x2, start=False, stop=False)
                    mm(ps, lo[:, a], x0, start=False, stop=False)
                    mm(ps, hi[:, r], x1, start=False, stop=False)
                    last = mm(ps, lo[0:D1, r], x1[0:D1, :], start=False, stop=True)
                    if f % 2:
                        last.then_inc(up, 1)

            def down_tile(q, p):
                hi, lo = views(p)
                pe.wait_ge(hid, q + 1)
                after(pe, biased, q - 1)
                for h in range(2):
                    ps = bank[5 + p][:, h * D:(h + 1) * D]
                    for f in range(FC):
                        c = slice(2 * F + f * D, 2 * F + (f + 1) * D)
                        n = slice(h * 128, (h + 1) * 128)
                        mm(ps, hh[p][:, f, n], hi[:, c], start=f == 0, stop=False)
                        mm(ps, hh[p][:, f, n], lo[:, c], start=False, stop=False)
                        last = mm(ps, hl[p][:, f, n], hi[:, c], start=False, stop=f == FC - 1)
                last.then_inc(down, 1)

            turn_rows(0, 0)

            def tiles(it):
                for p in range(2):
                    q = 2 * it + p
                    up_tile(it, p)
                    if not (isinstance(q, int) and q + 1 >= NT):
                        turn_rows(it + p, 1 - p)
                    if not (isinstance(q, int) and q == 0):
                        down_tile(q - 1, 1 - p)

            steps(pe, NT // 2, tiles, first=2, last=1)
            down_tile(NT - 1, 1)

        @block.scalar
        def _(act):
            f = nc.scalar.activation
            act.wait_ge(pos_t, 1)
            f(posT0[:, :], bank[1][:, 0:128], ACT.Copy)
            f(posT1[:, :], bank[1][0:D1, 128:256], ACT.Copy).then_inc(pos_ts, 1)
            for n in range(2):
                act.wait_ge(filt_arg, n + 1)
                f(sinb[:, 3 + n, :], sinb[:, 2, :], ACT.Sin).then_inc(filt_in, 1)
            act.wait_ge(cast_done, 1)
            act.wait_ge(loaded, 16 * N_LOADS)
            trow = cst[:, 512:640]
            f(dec[:, 0, :], trow, ACT.Exp, scale=filt[:, 0, 3:4])
            f(dec[0:D1, 1, :], trow[0:D1, :], ACT.Exp, scale=filt[0:D1, 1, 3:4]).then_inc(dec_done, 1)

            def quad(i, p):
                act.wait_ge(colsum, i + 1)
                f(col_s[:, :], bank[0][:, 0:GRAPHS * Q], ACT.Copy).then_inc(col_ready, 1)
                act.wait_ge(emb_t, i + 1)
                f(xt0[:, :], bank[1][:, :], ACT.Copy)
                f(xt1[0:D1, :], bank[2][0:D1, :], ACT.Copy).then_inc(xt_ready, 1)
                act.wait_ge(gvec, i + 1)
                f(gt_s[:, 0, :], bank[0][:, 64:64 + GRAPHS * Q], ACT.Copy)
                f(gt_s[0:D1, 1, :], bank[0][0:D1, 80:80 + GRAPHS * Q], ACT.Copy).then_inc(gvec_ready, 1)
                act.wait_ge(gfeat, i + 1)
                f(xt1[D1:PG, :].rearrange("p (b s) -> p b s", b=Q), repeat(bank[3][D1:PG, 0:Q], 2, 128), ACT.Relu,
                  bias=gbias[D1:PG, :]).then_inc(gfeat_ready, 1)

            def load_expert(e):
                act.dma_start(wst[:, :], t["wsrc"][bass.ds(e, 1), :, :].rearrange("e p x -> p (e x)")).then_inc(w_in, 16)
                act.dma_start(blob[:, WE:WE + FC], t["bi"][bass.ds(e, 1), :, :].rearrange("e p x -> p (e x)")).then_inc(w_in, 16)
                act.dma_start(blob[:, WE + FC:BLOB],
                              t["bo"][bass.ds(e, 1), :, :].rearrange("e o x -> o (e x)").to_broadcast([128, D])).then_inc(w_in, 16)

            def split_hi(e):
                act.wait_ge(w_in, 48 * (e + 1))
                f(blob[:, 0:WE // 2].bitcast(bf16), wst[:, :], ACT.Copy).then_inc(w_hi, 1)

            def store_expert(e):
                act.wait_ge(w_lo, e + 1)
                act.dma_start(blob_d[bass.ds(e, 1), :, :].rearrange("e p x -> p (e x)"), blob[:, :]).then_inc(w_out, 16)

            def quads(it):
                if not isinstance(it, int):
                    store_expert(it - 1)
                quad(2 * it, 0)
                after(act, w_out, 16 * it)
                load_expert(it)
                quad(2 * it + 1, 1)
                split_hi(it)

            steps(act, NQ // 2, quads)
            store_expert(E - 1)
            act.wait_ge(w_out, 16 * E)

            def turn(it):
                for s in range(RING):
                    c = it * RING + s
                    act.wait_ge(toep_in[s], 16 * (it + 1))
                    after(act, conv, c - 1)
                    f(tp[:, s % 2, :, :], reverse(toep[:, s, :, :]), ACT.Copy).then_inc(turned, 1)

            steps(act, NCH // RING, turn)

            def row_parts(i, p, first):
                act.wait_ge(ln_done, i + 1)
                if not first:
                    act.wait_ge(xrow_out[p], 8 * (i - p))
                f(xrow[:, p, :, 0:D], xn[:, p, :, :], ACT.Copy).then_inc(hi_done, 1)
                act.wait_ge(xn_t, i + 1)
                f(xnT0[:, :], bank[1][:, :], ACT.Copy)
                f(xnT1[:, :], bank[2][0:D1, :], ACT.Copy).then_inc(xnT_ready, 1)
                act.wait_ge(gap_ready, i + 1)
                f(wsm[:, 1, :], wsm[:, 0, :], ACT.Exp).then_inc(exp_done, 1)

            for p in range(2):
                row_parts(p, p, True)
            with act.Fori(1, NQ // 2) as it:
                for p in range(2):
                    row_parts(2 * it + p, p, False)

            def hidden(q, p, blocks):
                bi = wbuf[p][:, WE:WE + FC]
                for c in blocks:
                    act.wait_ge(up, FC // 2 * q + c // 2 + 1)
                    f(hf[p][:, c, :], bank[2 + c // 2][:, (c % 2) * TS:(c % 2 + 1) * TS], ACT.Gelu,
                      bias=bi[:, c:c + 1]).then_inc(gelu, 1)

            def tiles(it):
                for p in range(2):
                    q = 2 * it + p
                    after(act, hid, q - 1)
                    hidden(q, p, range(FC))

            steps(act, NT // 2, tiles, first=2)

        @block.vector
        def _(dve):
            v = nc.vector
            fence = dve.drain

            dve.wait_ge(loaded, 16 * N_LOADS)
            v.tensor_copy(ident[:, :], cst[:, 0:128])
            v.tensor_copy(identb[:, :], cst[:, 0:128])
            v.tensor_copy(tri[:, :], cst[:, 128:256])
            v.tensor_copy(iota_f[:, :], cst[:, 256:512])
            v.tensor_copy(iota_b[:, :], cst[:, 256:512])
            v.memset(ones_b[:, :], 1.0)
            v.memset(zero_f[:, :, :], 0.0)
            v.memset(mean_w[:, :], 1.0 / 128)
            v.memset(kT[:, :, S:NFFT], 0.0)
            for j in range(GRAPHS):
                for k in range(GRAPHS):
                    if k != j:
                        v.memset(wg[:, :, j, k * GD:(k + 1) * GD], 0.0)
            v.tensor_scalar(filt[:, 0, 3:4], filt[:, 0, 0:1], -1.0, None, ALU.mult)
            v.tensor_scalar(filt[0:D1, 1, 3:4], filt[0:D1, 1, 0:1], -1.0, None, ALU.mult).then_inc(cast_done, 1)

            def stage(i, p):
                v.tensor_copy(idx[:, p, :].rearrange("p (j b) -> p j b", b=Q), ids_i[:, :, bass.ds(i * Q, Q)]).then_inc(idx_staged, 1)

            stage(0, 0)
            stage(1, 1)
            cols = small[:, 32 + D:35 + D]
            for n in range(2):
                dve.wait_ge(filt_step, n + 1)
                fence()
                v.tensor_scalar(sinb[:, 0, :], bank[0][0:16, n * 128:(n + 1) * 128], cols[:, n:n + 1], cols[:, 2:3], ALU.add, ALU.mult)
                fence()
                v.tensor_scalar(sinb[:, 1, :], sinb[:, 0, :], 1.0 / TWO_PI, MAGIC, ALU.mult, ALU.add)
                fence()
                v.tensor_scalar(sinb[:, 1, :], sinb[:, 1, :], MAGIC, None, ALU.subtract)
                src = sinb[:, 0, :]
                if n:
                    dve.wait_ge(filt_in, n)
                for c in (C1, C2, C3):
                    fence()
                    v.scalar_tensor_tensor(sinb[:, 2, :], sinb[:, 1, :], -c, src, ALU.mult, ALU.add)
                    src = sinb[:, 2, :]
                fence()
                v.tensor_scalar(sinb[:, 2, :], sinb[:, 2, :], 3.1415925, -3.1415925, ALU.min, ALU.max).then_inc(filt_arg, 1)
            dve.wait_ge(filt_step, 3)
            dve.wait_ge(dec_done, 1)
            for c, n in ((0, D0), (1, D1)):
                kk = kT[0:n, c, 0:S]
                v.tensor_scalar(kk, bank[0][0:n, 256 + 128 * c:384 + 128 * c], filt[0:n, c, 1:2], 1.0 / NFFT, ALU.add, ALU.mult)
                fence()
                v.tensor_tensor(kk, kk, dec[0:n, c, :], ALU.mult)
                fence()
                v.tensor_tensor(kT[0:n, c, S - 1:S], kT[0:n, c, S - 1:S], filt[0:n, c, 2:3], ALU.add).then_inc(kready, 1)
            dve.wait_ge(pos_t, 2)
            v.tensor_tensor(posb[:, :], bank[2][:, 0:D], bproj[:, :], ALU.add).then_inc(pos_done, 1)

            def rsqrt(eps):
                v.tensor_scalar(rs[:, 1, :], mv[:, :, 1], eps, None, ALU.add)
                fence()
                v.tensor_scalar(rs[:, 0, :].bitcast(i32), rs[:, 1, :].bitcast(i32), 1, None, ALU.logical_shift_right)
                fence()
                v.tensor_scalar(rs[:, 0, :].bitcast(i32), rs[:, 0, :].bitcast(i32), -1.0, float(0x5F3759DF), ALU.mult, ALU.add)
                for _ in range(4):
                    fence()
                    v.tensor_tensor(rs[:, 2, :], rs[:, 0, :], rs[:, 0, :], ALU.mult)
                    fence()
                    v.tensor_tensor(rs[:, 2, :], rs[:, 2, :], rs[:, 1, :], ALU.mult)
                    fence()
                    v.tensor_scalar(rs[:, 2, :], rs[:, 2, :], -0.5, 1.5, ALU.mult, ALU.add)
                    fence()
                    v.tensor_tensor(rs[:, 0, :], rs[:, 0, :], rs[:, 2, :], ALU.mult)
                fence()

            def moments(src):
                for b in range(Q):
                    v.bn_stats(stats[:, b, :], src(b))
                fence()
                for b in range(Q):
                    v.bn_aggr(mv[:, b, :], stats[:, b, :])
                fence()

            def rows(i, p):
                dve.wait_ge(proj, i + 1)
                for h in range(2):
                    last = v.tensor_tensor(ys[:, 2 * h:2 * h + 2, :], bank[4 + h][:, 0:2 * D].rearrange("p (b d) -> p b d", b=2),
                                           repeat(posb[:, :], 1, 2), ALU.add)
                last.then_inc(proj_read, 1)
                fence()
                moments(lambda b: ys[:, b, :])
                rsqrt(EPS_TOK)
                for b in range(Q):
                    v.tensor_scalar(ys[:, b, :], ys[:, b, :], mv[:, b, 0:1], rs[:, 0, b:b + 1], ALU.subtract, ALU.mult)
                fence()
                v.tensor_tensor(ys[:, :, :], ys[:, :, :], repeat(gamma[:, :], 1, Q), ALU.mult)
                fence()
                v.tensor_tensor(ys[:, :, :], ys[:, :, :], repeat(beta[:, :], 1, Q), ALU.add)
                fence()
                v.tensor_copy(Hs[:, bass.ds(i * Q, Q), :], ys[:, :, :])
                moments(lambda b: ys[:, b, :])
                rsqrt(EPS_LN)
                for b in range(Q):
                    last = v.tensor_scalar(Ut[:, :, bass.ds(i * Q + b, 1)].rearrange("p c b -> p (c b)"), ys[:, b, :],
                                           mv[:, b, 0:1], rs[:, 0, b:b + 1], ALU.subtract, ALU.mult)
                last.then_inc(rows_done, 1)
                fence()

            def split_lo(e):
                dve.wait_ge(w_hi, e + 1)
                v.tensor_tensor(blob[:, WE // 2:WE].bitcast(bf16), wst[:, :], blob[:, 0:WE // 2].bitcast(bf16), ALU.subtract).then_inc(w_lo, 1)

            def quads(it):
                for p in range(2):
                    if not (isinstance(it, int) and it == NQ // 2 - 1):
                        dve.wait_ge(emb_in[p], 16 * Q * (it + 1))
                        dve.wait_ge(ev_in[p], 16 * GRAPHS * Q * (it + 1))
                        stage(2 * it + p + 2, p)
                    rows(2 * it + p, p)
                split_lo(it)

            steps(dve, NQ // 2, quads, first=0, last=1)

            def add_conv(it, s):
                c = it * RING + s
                dve.wait_ge(conv, c + 1)
                h = Hs[:, :, bass.ds(c * CC, CC)]
                v.tensor_tensor(h, h, bank[6 + s % 2][:, :].rearrange("p (c b) -> p b c", b=B), ALU.add).then_inc(conv_read, 1)

            fence()
            with dve.Fori(0, NCH // RING) as it:
                for s in range(RING):
                    add_conv(it, s)
            fence()

            def router(it, p, first):
                i = 2 * it + p
                h = lambda b: Hs[:, bass.ds(i * Q + b, 1), :].rearrange("p b d -> p (b d)")
                moments(h)
                rsqrt(EPS_LN)
                if not first:
                    dve.wait_ge(xn_t, i - 1)
                    dve.wait_ge(hi_done, i - 1)
                for b in range(Q):
                    last = v.tensor_scalar(xn[:, p, b, :], h(b), mv[:, b, 0:1], rs[:, 0, b:b + 1], ALU.subtract, ALU.mult)
                last.then_inc(ln_done, 1)
                fence()
                dve.wait_ge(hi_done, i + 1)
                v.tensor_tensor(xrow[:, p, :, D:D + D1], xn[:, p, :, D0:D], xrow[:, p, :, D0:D], ALU.subtract)
                v.tensor_tensor(xrow[:, p, :, D + D1:2 * D], xn[:, p, :, 0:D0], xrow[:, p, :, 0:D0], ALU.subtract)
                dve.wait_ge(logits, i + 1)
                v.tensor_copy(lg[:, :, :], bank[3][:, 0:Q * E].rearrange("p (b e) -> p b e", b=Q))
                fence()
                for b in range(Q):
                    v.max(top[:, b, :], lg[:, b, :])
                fence()
                v.tensor_tensor(wsm[:, 0, :], top[:, :, 1], top[:, :, 0], ALU.subtract).then_inc(gap_ready, 1)
                for b in range(Q):
                    v.max_index(topi[:, b, :], top[:, b, :], lg[:, b, :])
                fence()
                for k in range(2):
                    v.tensor_copy(e01[:, k, bass.ds(i * Q, Q)], topi[:, :, k])
                dve.wait_ge(exp_done, i + 1)
                v.tensor_scalar(wsm[:, 2, :], wsm[:, 1, :], 1.0, None, ALU.add)
                fence()
                v.reciprocal(wsm[:, 3, :], wsm[:, 2, :])
                fence()
                wr_ = xrow_f[:, p, :, D:D + 2]
                v.tensor_copy(wr_[:, :, 0], wsm[:, 3, :])
                v.tensor_tensor(wr_[:, :, 1], wsm[:, 1, :], wsm[:, 3, :], ALU.mult).then_inc(wts_done, 1)
                fence()

            for p in range(2):
                router(0, p, True)
            with dve.Fori(1, NQ // 2) as it:
                for p in range(2):
                    router(it, p, False)

            iota_e = bass.AP(tensor=iota_f, offset=0, ap=[[256, 128], [1, E], [0, B]])
            for k in range(2):
                v.tensor_tensor(oh[k], iota_e, repeat(e01[:, k, :], 1, E), ALU.is_equal)
            v.memset(onesf, 1.0)
            fence()
            v.tensor_tensor(ohb[:, :, :], oh[0], oh[1], ALU.add).then_inc(hot_ready, 1)
            dve.wait_ge(ranks, 1)
            tot = bank[5][:, :].rearrange("p (e b) -> p e b", e=E)
            for e in range(E):
                v.tensor_tensor_scan(run[:, e, :], onesf, tot[:, e, :], 0.0, ALU.mult, ALU.add)
            fence()
            v.tensor_copy(cnt[:, 0, :], run[:, :, B - 1])
            fence()
            v.tensor_scalar(cnt[:, 0, :], cnt[:, 0, :], float(TS - 1), None, ALU.add)
            fence()
            v.tensor_copy(cnti[:, 0, :], cnt[:, 0, :])
            fence()
            v.tensor_scalar(cnti[:, 1, :], cnti[:, 0, :], 8, None, ALU.logical_shift_right)
            fence()
            v.tensor_copy(cnt[:, 1, :], cnti[:, 1, :])
            fence()
            v.tensor_tensor_scan(cnt[:, 2, :], onesf[:, 0:E], cnt[:, 1, :], 0.0, ALU.mult, ALU.add)
            fence()
            v.tensor_tensor(cnt[:, 3, :], cnt[:, 2, :], cnt[:, 1, :], ALU.subtract)
            v.tensor_tensor(sl, run, tot, ALU.subtract)
            fence()
            v.tensor_tensor(sl, sl, bank[4][:, :].rearrange("p (e b) -> p e b", e=E), ALU.add)
            v.tensor_scalar(cnt[:, 3, :], cnt[:, 3, :], float(TS), None, ALU.mult)
            fence()
            v.tensor_tensor(sl, sl, repeat(cnt[:, 3, :], 2, B), ALU.add)
            fence()
            for k in range(2):
                v.tensor_tensor(oh[k], oh[k], sl, ALU.mult)
            fence()
            for k in range(2):
                v.tensor_reduce(slot[:, k, :], oh[k].rearrange("p e b -> p b e"), AX.X, ALU.add)
            fence()
            v.tensor_copy(sloti[:, 0, :, :], slot)
            fence()
            v.tensor_scalar(sloti[:, 1, :, :], sloti[:, 0, :, :], 7, None, ALU.logical_shift_right)
            v.tensor_scalar(sloti[:, 2, :, :], sloti[:, 0, :, :], 127, None, ALU.bitwise_and)
            fence()
            v.tensor_copy(slq, sloti[:, 1, :, :])
            v.tensor_copy(slp, sloti[:, 2, :, :])
            for k in range(2):
                v.tensor_scalar(tv[:, k:k + 1], cst[:, 640:641], float(1 + 128 * k), None, ALU.add)
            fence()

            def picks(it, first):
                for r in range(4):
                    b, k = 2 * it + r // 2, r % 2
                    if not first:
                        dve.wait_ge(pick_used, 4 * it + r - 3)
                    at_b = bass.ds(b, 1)
                    v.tensor_scalar(pick[:, r, 0, 0:128], iota_b[:, 0:128], slp[:, k, at_b], tv[:, k:k + 1], ALU.is_equal, ALU.mult)
                    v.tensor_scalar(pick[:, r, 1, 0:128], iota_b[:, 0:128], slp[:, k, at_b], iota_f[:, at_b], ALU.is_equal, ALU.mult)
                    v.tensor_scalar(pick[:, r, 2, 0:NC], iota_b[:, 0:NC], slq[:, k, at_b], None, ALU.is_equal).then_inc(pick_ready, 1)

            picks(0, True)
            with dve.Fori(1, B // 2) as it:
                picks(it, False)
            dve.wait_ge(table, 1)
            v.tensor_scalar(row_o, bank[6][:, 0:NC], 0.5, None, ALU.is_lt)
            v.tensor_scalar(row_k[:, :], bank[6][:, 0:NC], 128.5, None, ALU.is_gt)
            v.tensor_scalar(row_t, bank[6][:, 0:NC], 1.0, None, ALU.subtract)
            fence()
            v.scalar_tensor_tensor(row_t, row_k[:, :], -128.0, row_t, ALU.mult, ALU.add)
            v.tensor_scalar(id_f, bank[7][:, 0:NC], 128.0, None, ALU.mult)
            fence()
            v.tensor_tensor(id_f, id_f, row_t, ALU.add)
            fence()
            v.tensor_scalar(id_g[:, :], id_f, 0.0, None, ALU.max)
            v.tensor_tensor(row_o, row_o, cst[:, 641:641 + NC], ALU.mult)
            fence()
            v.tensor_tensor(id_s[:, :], id_f, row_o, ALU.add)
            iota_t = bass.AP(tensor=iota_f, offset=0, ap=[[256, 128], [1, NT], [0, E]])
            v.tensor_tensor(eidf, iota_t, repeat(cnt[:, 2, :], 1, NT), ALU.is_ge)
            fence()
            v.tensor_reduce(eidr, eidf, AX.X, ALU.add)
            fence()
            v.tensor_scalar(eid[:, :], eidr[0:1, :], float(E - 1), None, ALU.min)
            fence()
            dve.sem_inc(ids_done, 1)

            def stage_tile(q, p):
                c = bass.ds(2 * q, 2)
                v.tensor_copy(gi[:, p, :], id_g[:, c]).then_inc(stage_done, 1)

            def transposed(it, p):
                q = 2 * it + p
                dve.wait_ge(xg_t, q + 1)
                v.tensor_copy(xgT[:, p, :, :], bank[0][:, :].bitcast(bf16)[:, 0:3 * TS].rearrange("p (c n) -> p c n", c=3)).then_inc(xgT_ready, 1)

            def weights(q, p):
                w = xg_f[:, p, :, D:D + 2]
                fence()
                v.tensor_tensor(wk[:, p, :, 0], w[:, :, 1], w[:, :, 0], ALU.subtract)
                fence()
                v.tensor_tensor(wk[:, p, :, 0], wk[:, p, :, 0], row_k[:, bass.ds(2 * q, 2)], ALU.mult)
                fence()
                v.tensor_tensor(wk[:, p, :, 1], wk[:, p, :, 0], w[:, :, 0], ALU.add)
                fence()

            def split_hidden(q, p, blocks):
                for c in blocks:
                    dve.wait_ge(gelu, FC * q + c + 2)
                    v.tensor_copy(hh[p][:, c:c + 2, :], hf[p][:, c:c + 2, :])
                    fence()
                    last = v.tensor_tensor(hl[p][:, c:c + 2, :], hf[p][:, c:c + 2, :], hh[p][:, c:c + 2, :], ALU.subtract)
                return last

            def bias_out(q, p):
                for h in range(2):
                    after(dve, scat[h], 16 * (q - 1))
                dve.wait_ge(down, q + 1)
                v.tensor_copy(si[:, p, :], id_s[:, bass.ds(2 * q, 2)])
                v.tensor_tensor(yo[:, p, :, :], bank[5 + p][:, 0:2 * D].rearrange("p (h d) -> p h d", h=2),
                                repeat(wbuf[p][:, WE + FC:BLOB], 1, 2), ALU.add).then_inc(biased, 1)
                fence()
                for h in range(2):
                    last = v.tensor_scalar(yo[:, p, h, :], yo[:, p, h, :], wk[:, p, h, 1:2], None, ALU.mult)
                last.then_inc(yo_ready, 1)

            stage_tile(0, 0)
            stage_tile(1, 1)
            transposed(0, 0)

            def tiles(it):
                for p in range(2):
                    q = 2 * it + p
                    weights(q, p)
                    if not (isinstance(q, int) and q + 2 >= NT):
                        stage_tile(q + 2, p)
                    after(dve, down, q - 1)
                    split_hidden(q, p, (0, 2))
                    if not (isinstance(q, int) and q + 1 >= NT):
                        transposed(it + p, 1 - p)
                    split_hidden(q, p, (4,)).then_inc(hid, 1)
                    if not (isinstance(q, int) and q == 0):
                        bias_out(q - 1, 1 - p)

            steps(dve, NT // 2, tiles, first=2, last=1)
            bias_out(NT - 1, 1)


def kernel(**inputs):
    import numpy as np
    import concourse.bacc as bacc
    from concourse.bass_utils import run_bass_kernel_spmd

    a = {k: np.asarray(x) for k, x in inputs.items()}
    L = "L0_tok_"
    t = np.linspace(0.0, 1.0, S).astype(np.float32)
    w = 2.0 * np.pi * np.linspace(0.0, float(S - 1), S) / S
    zT = np.stack([t, np.cos(1e-4 * w), -np.sin(1e-4 * w)]).astype(np.float32)[:, ::-1]
    r = np.arange(128, dtype=np.float32)
    cst = np.concatenate([np.eye(128, dtype=np.float32), (r[:, None] < r[None, :]).astype(np.float32),
                          np.tile(np.arange(256, dtype=np.float32), (128, 1)), np.tile(t[::-1], (128, 1)), r[:, None],
                          (B * S + 1 + r[:, None] + 128 * (np.arange(NC) % 2)[None, :]).astype(np.float32)], axis=1)
    Wi, Wo = a["L0_ffn_Wi"], a["L0_ffn_Wo"]
    wiT = Wi.transpose(0, 2, 1)
    rest = wiT[:, D0:, :]
    wsrc = np.concatenate([wiT[:, :D0, :], np.concatenate([rest, rest], axis=1),
                           Wo.transpose(0, 2, 1).reshape(E, FC, 128, D).transpose(0, 2, 1, 3).reshape(E, 128, FC * D)], axis=2)
    ids = np.stack([a["x"], a["itok_BS_1_30519"], a["itok_BS_0_30521"], a["itok_BS_1_30520"]])
    col = lambda x: x[:, None]
    arrays = {
        "ids": ids.transpose(2, 0, 1).reshape(S, -1),
        "cst": cst,
        "adj0": a["fside_BSS_adj_cooc"], "adj1": a["fside_BSS_adj_het"], "adj2": a["fside_BSS_adj_isg"],
        "word_emb": a[L + "word_emb"], "pos": a[L + "pos_emb"], "WpT": a[L + "W_proj"].T,
        "b_proj": a[L + "b_proj"], "gamma": a[L + "ln_gamma"], "beta": a[L + "ln_beta"],
        "WgT": np.concatenate([a[L + "W_cooc"].T, a[L + "W_het"].T, a[L + "W_isg"].T], axis=1),
        "gbias": col(np.concatenate([a[L + "b_cooc"], a[L + "b_het"], a[L + "b_isg"]])),
        "WrT": a["L0_ffn_Wr"].T, "deltas": col(a["L0_attn_deltas_abs"]), "b3": col(a["L0_attn_b3"]),
        "bias": col(a["L0_attn_bias"]), "w1T": a["L0_attn_w1"].T, "w2T": a["L0_attn_w2"].T, "w3T": a["L0_attn_w3"].T,
        "cols": np.stack([a["L0_attn_b1"], a["L0_attn_b2"], a["L0_attn_freq"]], axis=1), "zT": zT,
        "wsrc": wsrc, "bi": a["L0_ffn_bi"].reshape(E, FC, 128).transpose(0, 2, 1), "bo": a["L0_ffn_bo"][:, None, :],
    }
    nc = bacc.Bacc("TRN2", target_bir_lowering=False, num_devices=1)
    feeds, handles = {}, {}
    for name, x in arrays.items():
        feeds[f"in_{name}"] = np.ascontiguousarray(x)
        handles[name] = nc.dram_tensor(f"in_{name}", x.shape, mybir.dt.from_np(x.dtype), kind="ExternalInput").ap()
    handles["adj"] = [handles[f"adj{j}"] for j in range(GRAPHS)]
    out = nc.dram_tensor("out_0", (B * S + SPARE, D), mybir.dt.float32, kind="ExternalOutput").ap()
    tower(nc, handles, out)
    res = run_bass_kernel_spmd(nc, [feeds], core_ids=[0])
    return res.results[0]["out_0"][0:B * S].reshape(B, S, D)
```

```python
from contextlib import ExitStack

import concourse.bass as bass
from concourse import mybir

B, S, D = 64, 128, 192
V = 30522
GRAPHS, GD = 3, 16
E, F = 8, 768
D0 = 128
D1 = D - D0
PG = D1 + GRAPHS * GD
Q = 4
NQ = B // Q
FC = F // 128
WE = 2 * F + FC * D
BLOB = WE + FC + D
XROW = 2 * D + 4
TS = 256
NT = 2 * B * S // TS + E
NC = NT * TS // 128
CC = 8
NCH = D // CC
RING = 4
P8 = 2 * Q
KG = GRAPHS * Q
GRP = 16
W3 = 3
PICKS = 4
NFFT = 2 * S
EPS_TOK, EPS_LN = 1e-12, 1e-5
TWO_PI = 6.283185307179586
C1 = 6.28125
C2 = 0.0019350051879882812
C3 = TWO_PI - C1 - C2
MAGIC = 12582912.0
SPARE = TS


def tower(nc, t, out):
    fp32, bf16, i32, u32 = mybir.dt.float32, mybir.dt.bfloat16, mybir.dt.int32, mybir.dt.uint32
    ALU, ACT, AX = mybir.AluOpType, mybir.ActivationFunctionType, mybir.AxisListType
    ctx = ExitStack()
    with ctx:
        def sb(name, shape, dt=fp32):
            return ctx.enter_context(nc.sbuf_tensor(name, shape, dt))

        def sem(name):
            return ctx.enter_context(nc.semaphore(name))

        def repeat(ap, at, n):
            dims = [list(d) for d in ap.ap]
            dims.insert(at, [0, n])
            return bass.AP(tensor=ap.tensor, offset=ap.offset, ap=dims)

        def reverse(ap):
            dims = [list(d) for d in ap.ap]
            step, n = dims[-1]
            dims[-1] = [-step, n]
            return bass.AP(tensor=ap.tensor, offset=ap.offset + step * (n - 1), ap=dims)

        def after(eng, semaphore, value):
            if not isinstance(value, int) or value > 0:
                eng.wait_ge(semaphore, value)

        def steps(eng, n, body, first=1, last=0):
            for it in range(first):
                body(it)
            with eng.Fori(first, n - last) as it:
                body(it)
            for it in range(n - last, n):
                body(it)

        out_rows = out[0:B * S, :].rearrange("(b s) d -> b s d", s=S)

        kpad_d = nc.dram_tensor("kpad_d", (D, NFFT), fp32).ap()
        xtab_d = nc.dram_tensor("xtab_d", (B * S, XROW // 2), fp32).ap()
        blob_d = nc.dram_tensor("blob_d", (E, 128, BLOB), fp32).ap()

        ident = sb("ident", [128, 128])
        identb = sb("identb", [128, 128], bf16)
        tri = sb("tri", [128, 128], bf16)
        ones_b = sb("ones_b", [128, 128], bf16)
        zero_f = sb("zero_f", [128, 2, D])
        iota_f = sb("iota_f", [128, 256])
        cst = sb("cst", [128, 128 + 128 + 256 + 128 + 1 + NC + 2 * B])
        mean_w = sb("mean_w", [128, 1])
        diag = sb("diag", [128, 2 * KG, 2 * KG])
        ids_i = sb("ids_i", [128, 1 + GRAPHS, B], i32)
        idx = sb("idx", [128, 2, Q * (1 + GRAPHS)], i32)
        wp0 = sb("wp0", [128, D])
        wp1 = sb("wp1", [PG, D])
        posb = sb("posb", [128, D])
        gamma = sb("gamma", [128, D])
        beta = sb("beta", [128, D])
        wg = sb("wg", [128, 2, GRAPHS, GRAPHS * GD])
        gbias = sb("gbias", [128, 1])
        wr = sb("wr", [128, 2, E])
        filt = sb("filt", [128, 2, 4])
        small = sb("small", [16, 3 + 16 + 16 + D + 128])
        kT = sb("kT", [128, 2, NFFT])

        emb_g = sb("emb_g", [128, 2, Q, D])
        ev_g = sb("ev_g", [128, 2, GRAPHS, Q, D])
        adj_s = sb("adj_s", [128, 2, GRAPHS, Q, 128])
        grow_s = sb("grow_s", [2 * KG, D])
        gt_s = sb("gt_s", [128, 2, 2 * KG])
        xt0 = sb("xt0", [128, P8 * 128])
        xt1 = sb("xt1", [128, P8 * 128])
        ys = sb("ys", [128, P8, D])
        start = ys[:, :, :].rearrange("p b d -> p (b d)")
        pos, bproj = start[:, 0:D], start[:, D:2 * D]
        posT0, posT1 = start[:, 2 * D:2 * D + 128], start[0:D1, 2 * D + 128:2 * D + 256]
        dec = start[:, 2 * D + 256:2 * D + 512].rearrange("p (c t) -> p c t", c=2)
        sinb = start[0:16, 2 * D + 512:2 * D + 1152].rearrange("p (n t) -> p n t", n=5)
        stats = sb("stats", [128, GRP, 6])
        mv = sb("mv", [128, GRP, 2])
        rs = sb("rs", [128, 3, GRP])
        ln1 = sb("ln1", [128, P8])
        ln2 = sb("ln2", [128, 2, P8])
        ln3 = sb("ln3", [128, 2, B])

        Hs = sb("Hs", [128, B, D])
        U = sb("U", [128, D * B])
        Ut = U[:, :].rearrange("p (c b) -> p c b", b=B)

        wst = sb("wst", [128, WE])
        blob = sb("blob", [128, BLOB])

        xn = U[:, 0:2 * Q * D].rearrange("p (a q d) -> p a q d", a=2, q=Q)
        xrow_f = U[:, 2 * Q * D:2 * Q * D + Q * XROW].rearrange("p (a q x) -> p a q x", a=2, q=Q)
        xrow = U[:, 2 * Q * D:2 * Q * D + Q * XROW].bitcast(bf16).rearrange("p (a q x) -> p a q x", a=2, q=Q)
        old_adj = adj_s[:, :, :, :, :].rearrange("p a j q h -> p (a j q h)")
        xnT0 = old_adj[:, 0:Q * 128]
        xnT1 = old_adj[0:D1, Q * 128:2 * Q * 128]
        lg = sb("lg", [128, Q, E])
        top = sb("top", [128, 2, Q, E])
        topi = sb("topi", [128, Q, E], u32)
        wsm = sb("wsm", [128, 2, 4, Q])
        e01 = sb("e01", [128, 2, B])

        rt = ev_g[:, :, :, :, :].rearrange("p a g q d -> p (a g q d)")
        toep = rt[:, 0:RING * CC * 128].rearrange("p (a c t) -> p a c t", a=RING, c=CC)
        at = [0]

        def carve(n):
            at[0] += n
            assert at[0] <= 2 * GRAPHS * Q * D
            return rt[:, at[0] - n:at[0]]

        oh = [carve(E * B).rearrange("p (e b) -> p e b", e=E) for _ in range(2)]
        sl = carve(E * B).rearrange("p (e b) -> p e b", e=E)
        run = carve(E * B).rearrange("p (e b) -> p e b", e=E)
        onesf = carve(B)
        ohb = sb("ohb", [128, E, B], bf16)
        cnt = carve(4 * E).rearrange("p (a e) -> p a e", a=4)
        slot = carve(2 * B).rearrange("p (b k) -> p b k", k=2)
        slq = carve(2 * B).rearrange("p (b k) -> p b k", k=2)
        slp = carve(2 * B).rearrange("p (b k) -> p b k", k=2)
        sloti = sb("sloti", [128, 3, B, 2], i32)
        cnti = sb("cnti", [128, 2, E], i32)
        row_k = sb("row_k", [128, NC])
        row_o = carve(NC)
        row_v = carve(2 * B).rearrange("p (b k) -> p b k", k=2)
        id_f = carve(NC)
        id_g = sb("id_g", [128, NC], i32)
        id_s = sb("id_s", [128, NC], i32)
        eidf = carve(NT * E).rearrange("p (t e) -> p t e", e=E)
        eidr = carve(NT)
        eid = sb("eid", [1, NT], i32)
        tp = wst[:, 0:2 * CC * 128].rearrange("p (a c t) -> p a c t", a=2, c=CC)
        hot_p = wst[:, 0:2 * PICKS * 128].rearrange("p (a r n) -> p a r n", a=2, r=PICKS)
        hot_q = wst[:, 2 * PICKS * 128:2 * PICKS * (128 + NC)].rearrange("p (a r n) -> p a r n", a=2, r=PICKS)

        wbuf = [U[:, w * BLOB:(w + 1) * BLOB] for w in range(W3)]
        flat = Hs[:, :, :].rearrange("p b d -> p (b d)")
        at_h = [0]

        def carve_h(n):
            at_h[0] += n
            assert at_h[0] <= D * B
            return flat[:, at_h[0] - n:at_h[0]]

        hf = [carve_h(FC * TS).rearrange("p (f n) -> p f n", f=FC) for _ in range(W3)]
        hh = [carve_h(FC * TS // 2).bitcast(bf16).rearrange("p (f n) -> p f n", f=FC) for _ in range(W3)]
        hl = [carve_h(FC * TS // 2).bitcast(bf16).rearrange("p (f n) -> p f n", f=FC) for _ in range(W3)]
        yo = carve_h(W3 * 2 * D).rearrange("p (a h d) -> p a h d", a=W3, h=2)
        xg_f = blob[:, 0:W3 * XROW].rearrange("p (a h x) -> p a h x", a=W3, h=2)
        xg = blob[:, 0:W3 * XROW].bitcast(bf16).rearrange("p (a h x) -> p a h x", a=W3, h=2)
        xgT = blob[:, 1200:1200 + W3 * 3 * TS // 2].bitcast(bf16).rearrange("p (a c n) -> p a c n", a=W3, c=3)
        gi = sb("gi", [128, W3, 2], i32)
        si = sb("si", [128, W3, 2], i32)
        wk = sb("wk", [128, W3, 2])

        bank = [ctx.enter_context(nc.psum_tensor(f"bank{i}", [128, 512], fp32)) for i in range(8)]

        loaded = sem("loaded")
        ids_in = sem("ids_in")
        cast_done = sem("cast_done")
        filt_step = sem("filt_step")
        filt_in = sem("filt_in")
        filt_arg = sem("filt_arg")
        kpad_stored = sem("kpad_stored")
        kready = sem("kready")
        dec_done = sem("dec_done")
        pos_done = sem("pos_done")
        pos_t = sem("pos_t")
        pos_ts = sem("pos_ts")
        adj_in = [sem(f"adj_in{p}") for p in range(2)]
        idx_staged = sem("idx_staged")
        emb_in = [sem(f"emb_in{p}") for p in range(2)]
        ev_in = [sem(f"ev_in{p}") for p in range(2)]
        pool_turn = sem("pool_turn")
        pe_turn = sem("pe_turn")
        colsum = sem("colsum")
        diag_ready = sem("diag_ready")
        emb_t = sem("emb_t")
        xt_ready = sem("xt_ready")
        gvec = sem("gvec")
        grow_ready = sem("grow_ready")
        gt = sem("gt")
        gt_ready = sem("gt_ready")
        gfeat = sem("gfeat")
        gfeat_ready = sem("gfeat_ready")
        proj = sem("proj")
        proj_read = sem("proj_read")
        ln_ready = sem("ln_ready")
        rows_done = sem("rows_done")
        moments_done = sem("moments_done")
        w_in = sem("w_in")
        w_hi = sem("w_hi")
        w_lo = sem("w_lo")
        w_out = sem("w_out")
        toep_in = [sem(f"toep_in{s}") for s in range(RING)]
        turned = sem("turned")
        conv = sem("conv")
        conv_read = sem("conv_read")
        ln_done = sem("ln_done")
        hi_done = sem("hi_done")
        lo_done = sem("lo_done")
        xrow_out = [sem(f"xrow_out{p}") for p in range(2)]
        h_out = sem("h_out")
        xn_t = sem("xn_t")
        xnT_ready = sem("xnT_ready")
        logits = sem("logits")
        gap_ready = sem("gap_ready")
        exp_done = sem("exp_done")
        wts_done = sem("wts_done")
        hot_ready = sem("hot_ready")
        ranks = sem("ranks")
        hots_ready = sem("hots_ready")
        pick_used = sem("pick_used")
        table = sem("table")
        ids_done = sem("ids_done")
        wb_in = [sem(f"wb_in{w}") for w in range(W3)]
        stage_done = sem("stage_done")
        xg_in = [sem(f"xg_in{w}") for w in range(W3)]
        xg_t = sem("xg_t")
        xgT_ready = sem("xgT_ready")
        up = sem("up")
        gelu = sem("gelu")
        hid = sem("hid")
        down = sem("down")
        biased = sem("biased")
        yo_ready = sem("yo_ready")
        scat = [sem(f"scat{h}") for h in range(2)]

        block = ctx.enter_context(nc.Block())

        N_LOADS = 27

        @block.sync
        def _(sp):
            n = [0]

            def load(dst, src):
                n[0] += 1
                sp.dma_start(dst, src).then_inc(loaded, 16)

            sp.dma_start(ids_i[:, :, :], t["ids"].rearrange("p (j b) -> p j b", j=1 + GRAPHS)).then_inc(ids_in, 16)
            load(cst[:, :], t["cst"])
            load(wp0[:, :], t["WpT"][0:D0, :])
            load(wp1[:, :], t["WpT"][D0:D0 + PG, :])
            load(pos[:, :], t["pos"])
            load(bproj[:, :], t["b_proj"].partition_broadcast(128))
            load(gamma[:, :], t["gamma"].partition_broadcast(128))
            load(beta[:, :], t["beta"].partition_broadcast(128))
            for j in range(GRAPHS):
                load(wg[:, 0, j, j * GD:(j + 1) * GD], t["WgT"][0:D0, j * GD:(j + 1) * GD])
                load(wg[0:D1, 1, j, j * GD:(j + 1) * GD], t["WgT"][D0:D, j * GD:(j + 1) * GD])
            load(gbias[D1:PG, :], t["gbias"])
            load(wr[:, 0, :], t["WrT"][0:D0, :])
            load(wr[0:D1, 1, :], t["WrT"][D0:D, :])
            for i, name in enumerate(("deltas", "b3", "bias")):
                load(filt[:, 0, i:i + 1], t[name][0:D0, :])
                load(filt[0:D1, 1, i:i + 1], t[name][D0:D, :])
            load(small[0:3, 0:16], t["w1T"])
            load(small[:, 16:32], t["w2T"])
            load(small[:, 32:32 + D], t["w3T"])
            load(small[:, 32 + D:32 + D + 3], t["cols"])
            load(small[0:3, 35 + D:35 + D + 128], t["zT"])
            assert n[0] == N_LOADS, n[0]

            def load_adj(i, p):
                for j in range(GRAPHS):
                    sp.dma_start(adj_s[:, p, j, :, :],
                                 t["adj"][j][bass.ds(i * Q, Q), :, :].rearrange("b g h -> g b h")).then_inc(adj_in[p], 16)

            load_adj(0, 0)
            load_adj(1, 1)
            with sp.Fori(0, NQ // 2 - 1) as it:
                for p in range(2):
                    sp.wait_ge(colsum, 2 * it + p + 1)
                    load_adj(2 * it + p + 2, p)

            sp.wait_ge(kready, 2)
            sp.dma_start(kpad_d[0:D0, :], kT[:, 0, :]).then_inc(kpad_stored, 16)
            sp.dma_start(kpad_d[D0:D, :], kT[0:D1, 1, :]).then_inc(kpad_stored, 16)
            sp.wait_ge(kpad_stored, 32)

            def load_toep(c, s):
                src = bass.AP(tensor=kpad_d.tensor, offset=c * (CC * NFFT), ap=[[1, 128], [NFFT, CC], [1, 128]])
                sp.dma_start(toep[:, s, :, :], src).then_inc(toep_in[s], 16)

            sp.wait_ge(gvec, NQ)
            for s in range(RING):
                load_toep(s, s)
            with sp.Fori(1, NCH // RING) as it:
                for s in range(RING):
                    sp.wait_ge(turned, it * RING + s + 1 - RING)
                    load_toep(it * RING + s, s)

            def store_rows(i, p):
                sp.dma_start(out_rows[bass.ds(i * Q, Q), :, :].rearrange("b s d -> s b d"),
                             Hs[:, bass.ds(i * Q, Q), :]).then_inc(h_out, 16)
                sp.wait_ge(wts_done, i + 1)
                sp.wait_ge(lo_done, i + 1)
                sp.dma_start(xtab_d[bass.ds(i * (Q * S), Q * S), :].rearrange("(b s) x -> s b x", s=S),
                             xrow_f[:, p, :, :]).then_inc(xrow_out[p], 16)

            sp.wait_ge(cast_done, 1)
            sp.dma_start(out[B * S:B * S + SPARE, :].rearrange("(a p) d -> p a d", a=2),
                         zero_f[:, :, :]).then_inc(h_out, 16)
            sp.wait_ge(conv_read, NCH)
            with sp.Fori(0, NQ // 2) as it:
                for p in range(2):
                    store_rows(2 * it + p, p)

            sp.wait_ge(w_out, 16 * E)
            for p in range(2):
                sp.wait_ge(xrow_out[p], 16 * (NQ // 2))
            sp.wait_ge(ids_done, 1)

            def expert(q):
                return sp.value_load(eid[0:1, bass.ds(q, 1)], min_val=0, max_val=E - 1)

            def load_w(e, w):
                sp.dma_start(wbuf[w], blob_d[bass.ds(e, 1), :, :].rearrange("e p x -> p (e x)")).then_inc(wb_in[w], 16)

            for w in range(W3):
                load_w(expert(w), w)
            with sp.Fori(1, NT // W3) as it:
                for w in range(W3):
                    q = W3 * it + w
                    sp.wait_ge(biased, q - W3 + 1)
                    e, held = expert(q), expert(q - W3)
                    with sp.If(e != held):
                        load_w(e, w)
                    with sp.Else():
                        sp.sem_inc(wb_in[w], 16)
            sp.wait_ge(h_out, 16 * (NQ + 1))
            for h in range(2):
                sp.wait_ge(scat[h], 16 * NT)

        @block.gpsimd
        def _(pool):
            def gathers(i, p):
                if not (isinstance(i, int) and i < 2):
                    pool.wait_ge(gvec, i - 1)
                nc.gpsimd.tensor_copy(idx[:, p, :].rearrange("p (j b) -> p j b", b=Q), ids_i[:, :, bass.ds(i * Q, Q)]).then_inc(idx_staged, 1)
                pool.wait_ge(idx_staged, i + 1)
                pool.sem_inc(pool_turn, 1)
                for b in range(Q):
                    pool.indirect_dma_start(emb_g[:, p, b, :], None, t["word_emb"],
                                            bass.IndirectOffsetOnAxis(ap=idx[:, p, b:b + 1], axis=0)).then_inc(emb_in[p], 16)
                for j in range(GRAPHS):
                    for b in range(Q):
                        k = (1 + j) * Q + b
                        pool.indirect_dma_start(ev_g[:, p, j, b, :], None, t["word_emb"],
                                                bass.IndirectOffsetOnAxis(ap=idx[:, p, k:k + 1], axis=0)).then_inc(ev_in[p], 16)

            pool.wait_ge(ids_in, 16)
            gathers(0, 0)
            gathers(1, 1)
            with pool.Fori(1, NQ // 2) as it:
                for p in range(2):
                    gathers(2 * it + p, p)

            def low(i, p):
                after(pool, xrow_out[p], 8 * (i - p))
                pool.wait_ge(hi_done, i + 1)
                nc.gpsimd.tensor_tensor(xrow[:, p, :, D:D + D1], xn[:, p, :, D0:D], xrow[:, p, :, D0:D], ALU.subtract)
                nc.gpsimd.tensor_tensor(xrow[:, p, :, D + D1:2 * D], xn[:, p, :, 0:D0], xrow[:, p, :, 0:D0], ALU.subtract).then_inc(lo_done, 1)

            def lows(it):
                for p in range(2):
                    low(2 * it + p, p)

            steps(pool, NQ // 2, lows)

            def fetch(q, w):
                pool.wait_ge(stage_done, q + 1)
                pool.sem_inc(pool_turn, 1)
                for h in range(2):
                    pool.indirect_dma_start(xg_f[:, w, h, :], None, xtab_d,
                                            bass.IndirectOffsetOnAxis(ap=gi[:, w, h:h + 1], axis=0)).then_inc(xg_in[w], 16)

            def add_rows(q, p):
                for h in range(2):
                    after(pool, scat[h], 16 * q)
                pool.wait_ge(yo_ready, q + 1)
                pool.sem_inc(pool_turn, 1)
                for h in range(2):
                    pool.indirect_dma_start(out, bass.IndirectOffsetOnAxis(ap=si[:, p, h:h + 1], axis=0), yo[:, p, h, :], None,
                                            compute_op=ALU.add).then_inc(scat[h], 16)

            for p in range(2):
                pool.wait_ge(xrow_out[p], 16 * (NQ // 2))
            pool.wait_ge(h_out, 16 * (NQ + 1))
            fetch(0, 0)
            fetch(1, 1)

            def tiles(it):
                for w in range(W3):
                    q = W3 * it + w
                    if not (isinstance(q, int) and q + 2 >= NT):
                        fetch(q + 2, (w + 2) % W3)
                    if not (isinstance(q, int) and q < 2):
                        add_rows(q - 2, (w + 1) % W3)

            steps(pool, NT // W3, tiles, last=1)
            for q in range(NT - 2, NT):
                add_rows(q, q % W3)

        @block.tensor
        def _(pe):
            mm = nc.tensor.matmul
            pe.wait_ge(loaded, 16 * N_LOADS)
            z = small[0:3, 35 + D:35 + D + 128]
            mm(bank[0][0:16, 0:128], small[0:3, 0:16], z, start=True, stop=True).then_inc(filt_step, 1)
            nc.tensor.transpose(bank[1][:, 0:128], pos[:, 0:D0], cst[:, 0:128])
            nc.tensor.transpose(bank[1][0:D1, 128:256], pos[:, D0:D], cst[:, 0:128]).then_inc(pos_t, 1)
            pe.wait_ge(pos_ts, 1)
            mm(bank[2][:, 0:D], posT0[:, :], wp0[:, :], start=True, stop=False)
            mm(bank[2][:, 0:D], posT1[:, :], wp1[0:D1, :], start=False, stop=True).then_inc(pos_t, 1)
            pe.wait_ge(filt_in, 1)
            mm(bank[0][0:16, 128:256], small[:, 16:32], sinb[:, 3, :], start=True, stop=True).then_inc(filt_step, 1)
            pe.wait_ge(filt_in, 2)
            mm(bank[0][:, 256:384], small[:, 32:32 + D0], sinb[:, 4, :], start=True, stop=True)
            mm(bank[0][0:D1, 384:512], small[:, 32 + D0:32 + D], sinb[:, 4, :], start=True, stop=True).then_inc(filt_step, 1)
            pe.wait_ge(kready, 2)
            pe.wait_ge(pos_done, 1)
            pe.wait_ge(cast_done, 1)

            def quad(it, p):
                i = 2 * it + p
                pe.wait_ge(adj_in[p], 16 * GRAPHS * (it + 1))
                for j in range(GRAPHS):
                    for b in range(Q):
                        k = p * KG + j * Q + b
                        last = mm(bank[0][:, k:k + 1], adj_s[:, p, j, b, :], mean_w[:, :], start=True, stop=True)
                last.then_inc(colsum, 1)
                after(pe, xt_ready, i)
                pe.wait_ge(emb_in[p], 16 * Q * (it + 1))
                for b in range(Q):
                    nc.tensor.transpose(bank[1][:, b * 128:(b + 1) * 128], emb_g[:, p, b, 0:D0], ident[:, :])
                    last = nc.tensor.transpose(bank[2][0:D1, b * 128:(b + 1) * 128], emb_g[:, p, b, D0:D], ident[:, :])
                last.then_inc(emb_t, 1)
                pe.wait_ge(diag_ready, i + 1)
                pe.wait_ge(ev_in[p], 16 * KG * (it + 1))
                for j in range(GRAPHS):
                    for b in range(Q):
                        k = p * KG + j * Q + b
                        last = mm(bank[3][0:2 * KG, 0:D], diag[:, k, :], ev_g[:, p, j, b, :],
                                  start=k == 0, stop=k == 2 * KG - 1)
                last.then_inc(gvec, 1)

            def pair(it):
                quad(it, 0)
                quad(it, 1)
                pe.wait_ge(grow_ready, it + 1)
                pe.sem_inc(pe_turn, 1)
                nc.tensor.transpose(bank[0][0:D1, 64:64 + 2 * KG], grow_s[:, D0:D], ident[0:2 * KG, 0:2 * KG])
                nc.tensor.transpose(bank[0][:, 32:32 + 2 * KG], grow_s[:, 0:D0], ident[0:2 * KG, 0:2 * KG]).then_inc(gt, 1)
                pe.wait_ge(gt_ready, it + 1)
                for j in range(GRAPHS):
                    for c, n in ((0, D0), (1, D1)):
                        g = gt_s[0:n, c, :].rearrange("p (a j b) -> p a j b", a=2, j=GRAPHS)[:, :, j, :]
                        last = mm(bank[3][D1:PG, 256:256 + P8], wg[0:n, c, j, :], g,
                                  start=j == 0 and c == 0, stop=j == GRAPHS - 1 and c == 1)
                last.then_inc(gfeat, 1)
                after(pe, proj_read, it)
                pe.wait_ge(xt_ready, 2 * it + 2)
                pe.wait_ge(gfeat_ready, it + 1)
                for b in range(P8):
                    ps = bank[4 + b // 2][:, (b % 2) * D:(b % 2 + 1) * D]
                    mm(ps, xt0[:, b * 128:(b + 1) * 128], wp0[:, :], start=True, stop=False)
                    last = mm(ps, xt1[0:PG, b * 128:(b + 1) * 128], wp1[:, :], start=False, stop=True)
                last.then_inc(proj, 1)

            steps(pe, NQ // 2, pair)

            pe.wait_ge(rows_done, NQ // 2)

            def chunk(it, s):
                c = it * RING + s
                pe.wait_ge(turned, c + 1)
                for k in range(CC):
                    n = 2 if k < CC - 1 else 1
                    last = mm(bank[6 + s % 2][:, k * B:(k + n) * B], tp[:, s % 2, k, :],
                              Ut[:, bass.ds(c * CC + k, n), :].rearrange("p c b -> p (c b)"), start=True, stop=True)
                last.then_inc(conv, 1)

            for s in range(RING):
                if s >= 2:
                    pe.wait_ge(conv_read, s - 1)
                chunk(0, s)
            with pe.Fori(1, NCH // RING) as it:
                for s in range(RING):
                    pe.wait_ge(conv_read, it * RING + s - 1)
                    chunk(it, s)

            def route(it, p):
                i = 2 * it + p
                pe.wait_ge(ln_done, i + 1)
                after(pe, xnT_ready, i)
                for b in range(Q):
                    nc.tensor.transpose(bank[1][:, b * 128:(b + 1) * 128], xn[:, p, b, 0:D0], ident[:, :])
                    last = nc.tensor.transpose(bank[2][0:D1, b * 128:(b + 1) * 128], xn[:, p, b, D0:D], ident[:, :])
                last.then_inc(xn_t, 1)
                pe.wait_ge(xnT_ready, i + 1)
                for b in range(Q):
                    ps = bank[3 + p][:, b * E:(b + 1) * E]
                    mm(ps, xnT0[:, b * 128:(b + 1) * 128], wr[:, 0, :], start=True, stop=False)
                    last = mm(ps, xnT1[:, b * 128:(b + 1) * 128], wr[0:D1, 1, :], start=False, stop=True)
                last.then_inc(logits, 1)

            def routes(it):
                for p in range(2):
                    after(pe, wts_done, 2 * it + p - 1)
                    route(it, p)

            steps(pe, NQ // 2, routes)

            pe.wait_ge(hot_ready, 1)
            hot = ohb[:, :, :].rearrange("p e b -> p (e b)")
            mm(bank[4][:, :], tri[:, :], hot, start=True, stop=True)
            mm(bank[5][:, :], ones_b[:, :], hot, start=True, stop=True).then_inc(ranks, 1)

            mm(bank[6][:, 0:NC], zero_f[:, 0, 0:128], iota_f[:, 0:NC], start=True, stop=False)
            with pe.Fori(0, B // PICKS) as it:
                for a in range(2):
                    pe.wait_ge(hots_ready, 2 * it + a + 1)
                    for r in range(PICKS):
                        last = mm(bank[6][:, 0:NC], hot_p[:, a, r, :], hot_q[:, a, r, :], start=False, stop=False)
                    last.then_inc(pick_used, 1)
            mm(bank[6][:, 0:NC], zero_f[:, 0, 0:128], iota_f[:, 0:NC], start=False, stop=True).then_inc(table, 1)
            pe.wait_ge(ids_done, 1)

            xT_ps = bank[0][:, :].bitcast(bf16)

            def views(p):
                w = wbuf[p]
                hi = w[:, 0:WE // 2].bitcast(bf16)
                lo = w[:, WE // 2:WE].bitcast(bf16)
                return hi, lo

            def turn_rows(it, w):
                pe.wait_ge(xg_in[w], 32 * (it + 1))
                for h in range(2):
                    for c in range(3):
                        last = nc.tensor.transpose(xT_ps[:, c * TS + h * 128:c * TS + h * 128 + 128],
                                                   xg[:, w, h, c * 128:(c + 1) * 128], identb[:, :])
                last.then_inc(xg_t, 1)

            def up_tile(it, w):
                q = W3 * it + w
                hi, lo = views(w)
                pe.wait_ge(xgT_ready, q + 1)
                pe.wait_ge(wb_in[w], 16 * (it + 1))
                x0, x1, x2 = (xgT[:, w, c, :] for c in range(3))
                for f in range(FC):
                    if f % 2 == 0:
                        after(pe, gelu, FC // 2 * (q - 1) + f // 2 + 1)
                    ps = bank[2 + f // 2][:, (f % 2) * TS:(f % 2 + 1) * TS]
                    a = slice(f * 128, (f + 1) * 128)
                    r = slice(F + f * 128, F + (f + 1) * 128)
                    mm(ps, hi[:, a], x0, start=True, stop=False)
                    mm(ps, hi[:, a], x2, start=False, stop=False)
                    mm(ps, lo[:, a], x0, start=False, stop=False)
                    mm(ps, hi[:, r], x1, start=False, stop=False)
                    last = mm(ps, lo[0:D1, r], x1[0:D1, :], start=False, stop=True)
                    if f % 2:
                        last.then_inc(up, 1)

            def down_tile(q, w):
                hi, lo = views(w)
                pe.wait_ge(hid, q + 1)
                after(pe, biased, q - W3 + 1)
                for h in range(2):
                    ps = bank[5 + w][:, h * D:(h + 1) * D]
                    for f in range(FC):
                        c = slice(2 * F + f * D, 2 * F + (f + 1) * D)
                        n = slice(h * 128, (h + 1) * 128)
                        mm(ps, hh[w][:, f, n], hi[:, c], start=f == 0, stop=False)
                        mm(ps, hh[w][:, f, n], lo[:, c], start=False, stop=False)
                        last = mm(ps, hl[w][:, f, n], hi[:, c], start=False, stop=f == FC - 1)
                last.then_inc(down, 1)

            turn_rows(0, 0)

            def tiles(it):
                for w in range(W3):
                    q = W3 * it + w
                    up_tile(it, w)
                    if not (isinstance(q, int) and q + 1 >= NT):
                        turn_rows(it + (w + 1) // W3, (w + 1) % W3)
                    if not (isinstance(q, int) and q == 0):
                        down_tile(q - 1, (w - 1) % W3)

            steps(pe, NT // W3, tiles, last=1)
            down_tile(NT - 1, (NT - 1) % W3)

        @block.scalar
        def _(act):
            f = nc.scalar.activation
            act.wait_ge(pos_t, 1)
            f(posT0[:, :], bank[1][:, 0:128], ACT.Copy)
            f(posT1[:, :], bank[1][0:D1, 128:256], ACT.Copy).then_inc(pos_ts, 1)
            for n in range(2):
                act.wait_ge(filt_arg, n + 1)
                f(sinb[:, 3 + n, :], sinb[:, 2, :], ACT.Sin).then_inc(filt_in, 1)
            act.wait_ge(cast_done, 1)
            act.wait_ge(loaded, 16 * N_LOADS)
            trow = cst[:, 512:640]
            f(dec[:, 0, :], trow, ACT.Exp, scale=filt[:, 0, 3:4])
            f(dec[0:D1, 1, :], trow[0:D1, :], ACT.Exp, scale=filt[0:D1, 1, 3:4]).then_inc(dec_done, 1)

            def quad(it, p):
                i = 2 * it + p
                act.wait_ge(colsum, i + 1)
                on_diag = bass.AP(tensor=diag, offset=p * KG * (2 * KG + 1), ap=[[4 * KG * KG, 128], [2 * KG + 1, KG]])
                f(on_diag, bank[0][:, p * KG:(p + 1) * KG], ACT.Copy).then_inc(diag_ready, 1)
                act.wait_ge(emb_t, i + 1)
                if p == 0:
                    after(act, proj, it)
                f(xt0[:, p * 512:(p + 1) * 512], bank[1][:, :], ACT.Copy)
                f(xt1[0:D1, p * 512:(p + 1) * 512], bank[2][0:D1, :], ACT.Copy).then_inc(xt_ready, 1)

            def graphs(it):
                act.wait_ge(gvec, 2 * it + 2)
                f(grow_s[:, :], bank[3][0:2 * KG, 0:D], ACT.Copy).then_inc(grow_ready, 1)
                act.wait_ge(gt, it + 1)
                f(gt_s[:, 0, :], bank[0][:, 32:32 + 2 * KG], ACT.Copy)
                f(gt_s[0:D1, 1, :], bank[0][0:D1, 64:64 + 2 * KG], ACT.Copy).then_inc(gt_ready, 1)
                act.wait_ge(gfeat, it + 1)
                f(xt1[D1:PG, :].rearrange("p (b s) -> p b s", b=P8), repeat(bank[3][D1:PG, 256:256 + P8], 2, 128), ACT.Relu,
                  bias=gbias[D1:PG, :]).then_inc(gfeat_ready, 1)

            def normal(it):
                act.wait_ge(ln_ready, it + 1)
                for b in range(P8):
                    last = f(Ut[:, :, bass.ds(it * P8 + b, 1)].rearrange("p c b -> p (c b)"),
                             Hs[:, bass.ds(it * P8 + b, 1), :].rearrange("p b d -> p (b d)"), ACT.Identity,
                             scale=ln2[:, 0, b:b + 1], bias=ln2[:, 1, b:b + 1])
                last.then_inc(rows_done, 1)

            def load_expert(e):
                act.dma_start(wst[:, :], t["wsrc"][bass.ds(e, 1), :, :].rearrange("e p x -> p (e x)")).then_inc(w_in, 16)
                act.dma_start(blob[:, WE:WE + FC], t["bi"][bass.ds(e, 1), :, :].rearrange("e p x -> p (e x)")).then_inc(w_in, 16)
                act.dma_start(blob[:, WE + FC:BLOB],
                              t["bo"][bass.ds(e, 1), :, :].rearrange("e o x -> o (e x)").to_broadcast([128, D])).then_inc(w_in, 16)

            def split_hi(e):
                act.wait_ge(w_in, 48 * (e + 1))
                f(blob[:, 0:WE // 2].bitcast(bf16), wst[:, :], ACT.Copy).then_inc(w_hi, 1)

            def store_expert(e):
                act.wait_ge(w_lo, e + 1)
                act.dma_start(blob_d[bass.ds(e, 1), :, :].rearrange("e p x -> p (e x)"), blob[:, :]).then_inc(w_out, 16)

            def pairs(it):
                first = isinstance(it, int)
                quad(it, 0)
                if not first:
                    split_hi(it - 1)
                quad(it, 1)
                graphs(it)
                if not first:
                    store_expert(it - 1)
                    normal(it - 1)
                    act.wait_ge(w_out, 16 * it)
                load_expert(it)

            steps(act, NQ // 2, pairs)
            normal(NQ // 2 - 1)
            split_hi(E - 1)
            store_expert(E - 1)
            act.wait_ge(w_out, 16 * E)

            def turn(it):
                for s in range(RING):
                    c = it * RING + s
                    act.wait_ge(toep_in[s], 16 * (it + 1))
                    after(act, conv, c - 1)
                    f(tp[:, s % 2, :, :], reverse(toep[:, s, :, :]), ACT.Copy).then_inc(turned, 1)

            steps(act, NCH // RING, turn)

            def row_parts(i, p):
                after(act, xn_t, i - 1)
                after(act, lo_done, i - 1)
                for b in range(Q):
                    last = f(xn[:, p, b, :], Hs[:, bass.ds(i * Q + b, 1), :].rearrange("p b d -> p (b d)"), ACT.Identity,
                             scale=ln3[:, 0, bass.ds(i * Q + b, 1)], bias=ln3[:, 1, bass.ds(i * Q + b, 1)])
                last.then_inc(ln_done, 1)
                after(act, xrow_out[p], 8 * (i - p))
                act.wait_ge(ln_done, i + 1)
                f(xrow[:, p, :, 0:D], xn[:, p, :, :], ACT.Copy).then_inc(hi_done, 1)

            def turned_parts(i, p):
                act.wait_ge(xn_t, i + 1)
                after(act, logits, i)
                f(xnT0[:, :], bank[1][:, :], ACT.Copy)
                f(xnT1[:, :], bank[2][0:D1, :], ACT.Copy).then_inc(xnT_ready, 1)

            def gap_exp(i, p):
                act.wait_ge(gap_ready, i + 1)
                f(wsm[:, p, 1, :], wsm[:, p, 0, :], ACT.Exp).then_inc(exp_done, 1)

            def quads4(g):
                act.wait_ge(moments_done, g + 1)
                for k in range(4):
                    i = 4 * g + k
                    row_parts(i, k % 2)
                    turned_parts(i, k % 2)
                    if not (isinstance(i, int) and i == 0):
                        gap_exp(i - 1, (k + 1) % 2)

            steps(act, NQ // 4, quads4)
            gap_exp(NQ - 1, 1)
            act.wait_ge(h_out, 16 * (NQ + 1))

            def hidden(q, w):
                bi = wbuf[w][:, WE:WE + FC]
                for c in range(0, FC, 2):
                    act.wait_ge(up, FC // 2 * q + c // 2 + 1)
                    for d in (c, c + 1):
                        ps = bank[2 + c // 2][:, (d % 2) * TS:(d % 2 + 1) * TS]
                        f(hh[w][:, d, :], ps, ACT.Gelu, bias=bi[:, d:d + 1])
                        last = f(hf[w][:, d, :], ps, ACT.Gelu, bias=bi[:, d:d + 1])
                    last.then_inc(gelu, 1)

            def tiles(it):
                for w in range(W3):
                    q = W3 * it + w
                    after(act, down, q - W3 + 1)
                    hidden(q, w)

            steps(act, NT // W3, tiles)

        @block.vector
        def _(dve):
            v = nc.vector
            fence = dve.drain

            dve.wait_ge(loaded, 16 * N_LOADS)
            v.tensor_copy(ident[:, :], cst[:, 0:128])
            v.tensor_copy(identb[:, :], cst[:, 0:128])
            v.tensor_copy(tri[:, :], cst[:, 128:256])
            v.tensor_copy(iota_f[:, :], cst[:, 256:512])
            v.memset(diag[:, :, :], 0.0)
            v.memset(ones_b[:, :], 1.0)
            v.memset(zero_f[:, :, :], 0.0)
            v.memset(mean_w[:, :], 1.0 / 128)
            v.memset(kT[:, :, S:NFFT], 0.0)
            for j in range(GRAPHS):
                for k in range(GRAPHS):
                    if k != j:
                        v.memset(wg[:, :, j, k * GD:(k + 1) * GD], 0.0)
            v.tensor_scalar(filt[:, 0, 3:4], filt[:, 0, 0:1], -1.0, None, ALU.mult)
            v.tensor_scalar(filt[0:D1, 1, 3:4], filt[0:D1, 1, 0:1], -1.0, None, ALU.mult).then_inc(cast_done, 1)

            cols = small[:, 32 + D:35 + D]
            for n in range(2):
                dve.wait_ge(filt_step, n + 1)
                fence()
                v.tensor_scalar(sinb[:, 0, :], bank[0][0:16, n * 128:(n + 1) * 128], cols[:, n:n + 1], cols[:, 2:3], ALU.add, ALU.mult)
                fence()
                v.tensor_scalar(sinb[:, 1, :], sinb[:, 0, :], 1.0 / TWO_PI, MAGIC, ALU.mult, ALU.add)
                fence()
                v.tensor_scalar(sinb[:, 1, :], sinb[:, 1, :], MAGIC, None, ALU.subtract)
                src = sinb[:, 0, :]
                if n:
                    dve.wait_ge(filt_in, n)
                for c in (C1, C2, C3):
                    fence()
                    v.scalar_tensor_tensor(sinb[:, 2, :], sinb[:, 1, :], -c, src, ALU.mult, ALU.add)
                    src = sinb[:, 2, :]
                fence()
                v.tensor_scalar(sinb[:, 2, :], sinb[:, 2, :], 3.1415925, -3.1415925, ALU.min, ALU.max).then_inc(filt_arg, 1)
            dve.wait_ge(filt_step, 3)
            dve.wait_ge(dec_done, 1)
            for c, n in ((0, D0), (1, D1)):
                kk = kT[0:n, c, 0:S]
                v.tensor_scalar(kk, bank[0][0:n, 256 + 128 * c:384 + 128 * c], filt[0:n, c, 1:2], 1.0 / NFFT, ALU.add, ALU.mult)
                fence()
                v.tensor_tensor(kk, kk, dec[0:n, c, :], ALU.mult)
                fence()
                v.tensor_tensor(kT[0:n, c, S - 1:S], kT[0:n, c, S - 1:S], filt[0:n, c, 2:3], ALU.add).then_inc(kready, 1)
            dve.wait_ge(pos_t, 2)
            v.tensor_tensor(posb[:, :], bank[2][:, 0:D], bproj[:, :], ALU.add).then_inc(pos_done, 1)

            def rsqrt(n, out_ap, eps):
                y, t, x = rs[:, 0, 0:n], rs[:, 1, 0:n], rs[:, 2, 0:n]
                v.tensor_scalar(x, mv[:, 0:n, 1], eps, None, ALU.add)
                fence()
                v.tensor_scalar(y.bitcast(i32), x.bitcast(i32), 1, None, ALU.logical_shift_right)
                v.tensor_scalar(x, x, -0.5, None, ALU.mult)
                fence()
                v.tensor_scalar(y.bitcast(i32), y.bitcast(i32), -1.0, float(0x5F3759DF), ALU.mult, ALU.add)
                for step in range(3):
                    fence()
                    v.tensor_tensor(t, y, y, ALU.mult)
                    fence()
                    v.tensor_tensor(t, t, x, ALU.mult)
                    fence()
                    v.scalar_tensor_tensor(out_ap if step == 2 else y, t, 1.5, y, ALU.add, ALU.mult)
                fence()

            def moments(n, src):
                for b in range(n):
                    v.bn_stats(stats[:, b, :], src(b))
                fence()
                for b in range(n):
                    v.bn_aggr(mv[:, b, :], stats[:, b, :])
                fence()

            def rows(it):
                dve.wait_ge(proj, it + 1)
                for h in range(P8 // 2):
                    last = v.tensor_tensor(ys[:, 2 * h:2 * h + 2, :], bank[4 + h][:, 0:2 * D].rearrange("p (b d) -> p b d", b=2),
                                           repeat(posb[:, :], 1, 2), ALU.add)
                last.then_inc(proj_read, 1)
                fence()
                moments(P8, lambda b: ys[:, b, :])
                rsqrt(P8, ln1[:, :], EPS_TOK)
                h = lambda b: Hs[:, bass.ds(it * P8 + b, 1), :].rearrange("p b d -> p (b d)")
                for b in range(P8):
                    v.scalar_tensor_tensor(ys[:, b, :], ys[:, b, :], mv[:, b, 0:1], gamma[:, :], ALU.subtract, ALU.mult)
                fence()
                for b in range(P8):
                    v.scalar_tensor_tensor(h(b), ys[:, b, :], ln1[:, b:b + 1], beta[:, :], ALU.mult, ALU.add)
                fence()
                moments(P8, h)
                after(dve, rows_done, it)
                rsqrt(P8, ln2[:, 0, :], EPS_LN)
                v.scalar_tensor_tensor(ln2[:, 1, :], mv[:, 0:P8, 0], -1.0, ln2[:, 0, :], ALU.mult, ALU.mult).then_inc(ln_ready, 1)
                fence()

            def split_lo(e):
                dve.wait_ge(w_hi, e + 1)
                v.tensor_tensor(blob[:, WE // 2:WE].bitcast(bf16), wst[:, :], blob[:, 0:WE // 2].bitcast(bf16), ALU.subtract).then_inc(w_lo, 1)

            def pairs(it):
                rows(it)
                split_lo(it)

            steps(dve, NQ // 2, pairs)

            def add_conv(it, s):
                c = it * RING + s
                dve.wait_ge(conv, c + 1)
                h = Hs[:, :, bass.ds(c * CC, CC)]
                v.tensor_tensor(h, h, bank[6 + s % 2][:, :].rearrange("p (c b) -> p b c", b=B), ALU.add).then_inc(conv_read, 1)

            fence()
            with dve.Fori(0, NCH // RING) as it:
                for s in range(RING):
                    add_conv(it, s)
            fence()

            def group_moments(g):
                moments(GRP, lambda b: Hs[:, bass.ds(g * GRP + b, 1), :].rearrange("p b d -> p (b d)"))
                at_g = bass.ds(g * GRP, GRP)
                rsqrt(GRP, ln3[:, 0, at_g], EPS_LN)
                v.scalar_tensor_tensor(ln3[:, 1, at_g], mv[:, :, 0], -1.0, ln3[:, 0, at_g], ALU.mult, ALU.mult).then_inc(moments_done, 1)
                fence()

            def choices(i, p):
                dve.wait_ge(logits, i + 1)
                v.tensor_copy(lg[:, :, :], bank[3 + p][:, 0:Q * E].rearrange("p (b e) -> p b e", b=Q))
                fence()
                for b in range(Q):
                    v.max(top[:, p, b, :], lg[:, b, :])
                fence()
                v.tensor_tensor(wsm[:, p, 0, :], top[:, p, :, 1], top[:, p, :, 0], ALU.subtract).then_inc(gap_ready, 1)
                for b in range(Q):
                    v.max_index(topi[:, b, :], top[:, p, b, :], lg[:, b, :])
                fence()
                for k in range(2):
                    v.tensor_copy(e01[:, k, bass.ds(i * Q, Q)], topi[:, :, k])

            def shares(i, p):
                dve.wait_ge(exp_done, i + 1)
                v.tensor_scalar(wsm[:, p, 2, :], wsm[:, p, 1, :], 1.0, None, ALU.add)
                fence()
                v.reciprocal(wsm[:, p, 3, :], wsm[:, p, 2, :])
                fence()
                after(dve, xrow_out[p], 8 * (i - p))
                v.tensor_copy(xrow_f[:, p, :, D], wsm[:, p, 3, :])
                v.scalar_tensor_tensor(xrow_f[:, p, :, D + 1], wsm[:, p, 1, :], 1.0, wsm[:, p, 3, :], ALU.subtract, ALU.mult).then_inc(wts_done, 1)

            group_moments(0)

            def groups(g):
                if not (isinstance(g, int) and g == NQ // 4 - 1):
                    group_moments(g + 1)
                for k in range(4):
                    i = 4 * g + k
                    choices(i, k % 2)
                    if not (isinstance(i, int) and i == 0):
                        shares(i - 1, (k + 1) % 2)

            steps(dve, NQ // 4, groups, last=1)
            shares(NQ - 1, 1)
            fence()

            iota_e = bass.AP(tensor=iota_f, offset=0, ap=[[256, 128], [1, E], [0, B]])
            for k in range(2):
                v.tensor_tensor(oh[k], iota_e, repeat(e01[:, k, :], 1, E), ALU.is_equal)
            v.memset(onesf, 1.0)
            fence()
            v.tensor_tensor(ohb[:, :, :], oh[0], oh[1], ALU.add).then_inc(hot_ready, 1)
            dve.wait_ge(ranks, 1)
            tot = bank[5][:, :].rearrange("p (e b) -> p e b", e=E)
            for e in range(E):
                v.tensor_tensor_scan(run[:, e, :], onesf, tot[:, e, :], 0.0, ALU.mult, ALU.add)
            fence()
            v.tensor_copy(cnt[:, 0, :], run[:, :, B - 1])
            fence()
            v.tensor_scalar(cnt[:, 0, :], cnt[:, 0, :], float(TS - 1), None, ALU.add)
            fence()
            v.tensor_copy(cnti[:, 0, :], cnt[:, 0, :])
            fence()
            v.tensor_scalar(cnti[:, 1, :], cnti[:, 0, :], 8, None, ALU.logical_shift_right)
            fence()
            v.tensor_copy(cnt[:, 1, :], cnti[:, 1, :])
            fence()
            v.tensor_tensor_scan(cnt[:, 2, :], onesf[:, 0:E], cnt[:, 1, :], 0.0, ALU.mult, ALU.add)
            fence()
            v.tensor_tensor(cnt[:, 3, :], cnt[:, 2, :], cnt[:, 1, :], ALU.subtract)
            v.tensor_tensor(sl, run, tot, ALU.subtract)
            fence()
            v.tensor_tensor(sl, sl, bank[4][:, :].rearrange("p (e b) -> p e b", e=E), ALU.add)
            v.tensor_scalar(cnt[:, 3, :], cnt[:, 3, :], float(TS), None, ALU.mult)
            fence()
            v.tensor_tensor(sl, sl, repeat(cnt[:, 3, :], 2, B), ALU.add)
            fence()
            for k in range(2):
                v.tensor_tensor(oh[k], oh[k], sl, ALU.mult)
            fence()
            for k in range(2):
                v.tensor_reduce(slot[:, :, k], oh[k].rearrange("p e b -> p b e"), AX.X, ALU.add)
            v.tensor_copy(row_v, cst[:, 641 + NC:641 + NC + 2 * B].rearrange("p (b k) -> p b k", k=2))
            fence()
            v.tensor_copy(sloti[:, 0, :, :], slot)
            fence()
            v.tensor_scalar(sloti[:, 1, :, :], sloti[:, 0, :, :], 7, None, ALU.logical_shift_right)
            v.tensor_scalar(sloti[:, 2, :, :], sloti[:, 0, :, :], 127, None, ALU.bitwise_and)
            fence()
            v.tensor_copy(slq, sloti[:, 1, :, :])
            v.tensor_copy(slp, sloti[:, 2, :, :])
            fence()
            def hots(it):
                for a in range(2):
                    n = 2 * it + a
                    after(dve, pick_used, n - 1)
                    rows_of = slp[:, bass.ds(n * (PICKS // 2), PICKS // 2), :].rearrange("p b k -> p (b k)")
                    v.tensor_tensor(hot_p[:, a, :, :], repeat(iota_f[:, 0:128], 1, PICKS),
                                    rows_of.unsqueeze(2).to_broadcast([128, PICKS, 128]), ALU.is_equal)
                    for r in range(PICKS):
                        b, k = bass.ds(n * (PICKS // 2) + r // 2, 1), r % 2
                        last = v.tensor_scalar(hot_q[:, a, r, :], iota_f[:, 0:NC], slq[:, b, k], row_v[:, b, k], ALU.is_equal, ALU.mult)
                    last.then_inc(hots_ready, 1)

            steps(dve, B // PICKS, hots)
            dve.wait_ge(table, 1)
            v.tensor_scalar(row_o, bank[6][:, 0:NC], 0.5, None, ALU.is_lt)
            v.tensor_scalar(row_k[:, :], bank[6][:, 0:NC], B * S + 0.5, None, ALU.is_gt)
            v.tensor_scalar(id_f, bank[6][:, 0:NC], 1.0, None, ALU.subtract)
            fence()
            v.scalar_tensor_tensor(id_f, row_k[:, :], -float(B * S), id_f, ALU.mult, ALU.add)
            fence()
            v.tensor_scalar(id_g[:, :], id_f, 0.0, None, ALU.max)
            v.tensor_tensor(row_o, row_o, cst[:, 641:641 + NC], ALU.mult)
            fence()
            v.tensor_tensor(id_s[:, :], id_f, row_o, ALU.add)
            iota_t = bass.AP(tensor=iota_f, offset=0, ap=[[256, 128], [1, NT], [0, E]])
            v.tensor_tensor(eidf, iota_t, repeat(cnt[:, 2, :], 1, NT), ALU.is_ge)
            fence()
            v.tensor_reduce(eidr, eidf, AX.X, ALU.add)
            fence()
            v.tensor_scalar(eid[:, :], eidr[0:1, :], float(E - 1), None, ALU.min)
            fence()
            dve.sem_inc(ids_done, 1)

            def stage_tile(q, w):
                v.tensor_copy(gi[:, w, :], id_g[:, bass.ds(2 * q, 2)]).then_inc(stage_done, 1)

            def transposed(q, w):
                dve.wait_ge(xg_t, q + 1)
                v.tensor_copy(xgT[:, w, :, :], bank[0][:, :].bitcast(bf16)[:, 0:3 * TS].rearrange("p (c n) -> p c n", c=3)).then_inc(xgT_ready, 1)

            def weights(q, w):
                for h in range(2):
                    v.scalar_tensor_tensor(wk[:, w, h:h + 1], xg_f[:, w, h, D + 1:D + 2], row_k[:, bass.ds(2 * q + h, 1)],
                                           xg_f[:, w, h, D:D + 1], ALU.mult, ALU.add)

            def split_hidden(q, w, blocks):
                for c in blocks:
                    dve.wait_ge(gelu, FC // 2 * q + c // 2 + 1)
                    last = v.tensor_tensor(hl[w][:, c:c + 2, :], hf[w][:, c:c + 2, :], hh[w][:, c:c + 2, :], ALU.subtract)
                return last

            def bias_out(q, w):
                for h in range(2):
                    after(dve, scat[h], 16 * (q - W3 + 1))
                dve.wait_ge(down, q + 1)
                v.tensor_copy(si[:, w, :], id_s[:, bass.ds(2 * q, 2)])
                v.tensor_tensor(yo[:, w, :, :], bank[5 + w][:, 0:2 * D].rearrange("p (h d) -> p h d", h=2),
                                repeat(wbuf[w][:, WE + FC:BLOB], 1, 2), ALU.add).then_inc(biased, 1)
                fence()
                for h in range(2):
                    last = v.tensor_scalar(yo[:, w, h, :], yo[:, w, h, :], wk[:, w, h:h + 1], None, ALU.mult)
                last.then_inc(yo_ready, 1)

            dve.wait_ge(h_out, 16 * (NQ + 1))
            stage_tile(0, 0)
            stage_tile(1, 1)
            transposed(0, 0)

            def tiles(it):
                for w in range(W3):
                    q = W3 * it + w
                    weights(q, w)
                    if not (isinstance(q, int) and q + 2 >= NT):
                        stage_tile(q + 2, (w + 2) % W3)
                    after(dve, down, q - W3 + 1)
                    split_hidden(q, w, (0, 2))
                    if not (isinstance(q, int) and q + 1 >= NT):
                        transposed(q + 1, (w + 1) % W3)
                    split_hidden(q, w, (4,)).then_inc(hid, 1)
                    if not (isinstance(q, int) and q == 0):
                        bias_out(q - 1, (w - 1) % W3)

            steps(dve, NT // W3, tiles, last=1)
            bias_out(NT - 1, (NT - 1) % W3)


def kernel(**inputs):
    import numpy as np
    import concourse.bacc as bacc
    from concourse.bass_utils import run_bass_kernel_spmd

    a = {k: np.asarray(x) for k, x in inputs.items()}
    L = "L0_tok_"
    t = np.linspace(0.0, 1.0, S).astype(np.float32)
    w = 2.0 * np.pi * np.linspace(0.0, float(S - 1), S) / S
    zT = np.stack([t, np.cos(1e-4 * w), -np.sin(1e-4 * w)]).astype(np.float32)[:, ::-1]
    r = np.arange(128, dtype=np.float32)
    cst = np.concatenate([np.eye(128, dtype=np.float32), (r[:, None] < r[None, :]).astype(np.float32),
                          np.tile(np.arange(256, dtype=np.float32), (128, 1)), np.tile(t[::-1], (128, 1)), r[:, None],
                          (B * S + 1 + r[:, None] + 128 * (np.arange(NC) % 2)[None, :]).astype(np.float32),
                          (1 + r[:, None, None] + S * np.arange(B)[None, :, None] + B * S * np.arange(2)[None, None, :])
                          .reshape(128, 2 * B).astype(np.float32)], axis=1)
    Wi, Wo = a["L0_ffn_Wi"], a["L0_ffn_Wo"]
    wiT = Wi.transpose(0, 2, 1)
    rest = wiT[:, D0:, :]
    wsrc = np.concatenate([wiT[:, :D0, :], np.concatenate([rest, rest], axis=1),
                           Wo.transpose(0, 2, 1).reshape(E, FC, 128, D).transpose(0, 2, 1, 3).reshape(E, 128, FC * D)], axis=2)
    ids = np.stack([a["x"], a["itok_BS_1_30519"], a["itok_BS_0_30521"], a["itok_BS_1_30520"]])
    col = lambda x: x[:, None]
    arrays = {
        "ids": ids.transpose(2, 0, 1).reshape(S, -1),
        "cst": cst,
        "adj0": a["fside_BSS_adj_cooc"], "adj1": a["fside_BSS_adj_het"], "adj2": a["fside_BSS_adj_isg"],
        "word_emb": a[L + "word_emb"], "pos": a[L + "pos_emb"], "WpT": a[L + "W_proj"].T,
        "b_proj": a[L + "b_proj"], "gamma": a[L + "ln_gamma"], "beta": a[L + "ln_beta"],
        "WgT": np.concatenate([a[L + "W_cooc"].T, a[L + "W_het"].T, a[L + "W_isg"].T], axis=1),
        "gbias": col(np.concatenate([a[L + "b_cooc"], a[L + "b_het"], a[L + "b_isg"]])),
        "WrT": a["L0_ffn_Wr"].T, "deltas": col(a["L0_attn_deltas_abs"]), "b3": col(a["L0_attn_b3"]),
        "bias": col(a["L0_attn_bias"]), "w1T": a["L0_attn_w1"].T, "w2T": a["L0_attn_w2"].T, "w3T": a["L0_attn_w3"].T,
        "cols": np.stack([a["L0_attn_b1"], a["L0_attn_b2"], a["L0_attn_freq"]], axis=1), "zT": zT,
        "wsrc": wsrc, "bi": a["L0_ffn_bi"].reshape(E, FC, 128).transpose(0, 2, 1), "bo": a["L0_ffn_bo"][:, None, :],
    }
    nc = bacc.Bacc("TRN2", target_bir_lowering=False, num_devices=1)
    feeds, handles = {}, {}
    for name, x in arrays.items():
        feeds[f"in_{name}"] = np.ascontiguousarray(x)
        handles[name] = nc.dram_tensor(f"in_{name}", x.shape, mybir.dt.from_np(x.dtype), kind="ExternalInput").ap()
    handles["adj"] = [handles[f"adj{j}"] for j in range(GRAPHS)]
    out = nc.dram_tensor("out_0", (B * S + SPARE, D), mybir.dt.float32, kind="ExternalOutput").ap()
    tower(nc, handles, out)
    res = run_bass_kernel_spmd(nc, [feeds], core_ids=[0])
    return res.results[0]["out_0"][0:B * S].reshape(B, S, D)
```

```python
from contextlib import ExitStack

import concourse.bass as bass
from concourse import mybir

B, S, D = 64, 128, 192
V = 30522
GRAPHS, GD = 3, 16
E, F = 8, 768
D0 = 128
D1 = D - D0
PG = D1 + GRAPHS * GD
Q = 4
NQ = B // Q
FC = F // 128
WI, WO = 2 * F, FC * D
WE = WI + WO
UP, DOWN = WI + FC, WO + D
BLOB = UP + DOWN
XROW = 2 * D + 4
TS = 256
NT = (2 * B * S + E * (TS - 1)) // TS
NC = NT * TS // 128
CC = 8
NCH = D // CC
RING = 4
KG = GRAPHS * Q
QG = 4
GRP = QG * Q
NG = NQ // QG
W3 = 3
ROUNDS = -(-NT // W3)
PICKS = 8
NFFT = 2 * S
EPS_TOK, EPS_LN = 1e-12, 1e-5
TWO_PI = 6.283185307179586
C1 = 6.28125
C2 = 0.0019350051879882812
C3 = TWO_PI - C1 - C2
MAGIC = 12582912.0
SPARE = TS


def tower(nc, t, out):
    fp32, bf16, i32, u32 = mybir.dt.float32, mybir.dt.bfloat16, mybir.dt.int32, mybir.dt.uint32
    ALU, ACT, AX = mybir.AluOpType, mybir.ActivationFunctionType, mybir.AxisListType
    ctx = ExitStack()
    with ctx:
        def sb(name, shape, dt=fp32):
            return ctx.enter_context(nc.sbuf_tensor(name, shape, dt))

        def sem(name):
            return ctx.enter_context(nc.semaphore(name))

        def repeat(ap, at, n):
            dims = [list(d) for d in ap.ap]
            dims.insert(at, [0, n])
            return bass.AP(tensor=ap.tensor, offset=ap.offset, ap=dims)

        def reverse(ap):
            dims = [list(d) for d in ap.ap]
            step, n = dims[-1]
            dims[-1] = [-step, n]
            return bass.AP(tensor=ap.tensor, offset=ap.offset + step * (n - 1), ap=dims)

        def after(eng, semaphore, value):
            if not isinstance(value, int) or value > 0:
                eng.wait_ge(semaphore, value)

        def steps(eng, n, body, first=1, last=0):
            for it in range(first):
                body(it)
            with eng.Fori(first, n - last) as it:
                body(it)
            for it in range(n - last, n):
                body(it)

        out_rows = out[0:B * S, :].rearrange("(b s) d -> b s d", s=S)

        kpad_d = nc.dram_tensor("kpad_d", (D, NFFT), fp32).ap()
        xtab_d = nc.dram_tensor("xtab_d", (B * S, XROW // 2), fp32).ap()
        blob_d = nc.dram_tensor("blob_d", (E, 128, BLOB), fp32).ap()

        def parts(room):
            up_w, down_w = room[:, 0:UP], room[:, UP:BLOB]
            return (up_w[:, 0:WI // 2].bitcast(bf16), up_w[:, WI // 2:WI].bitcast(bf16), up_w[:, WI:UP],
                    down_w[:, 0:WO // 2].bitcast(bf16), down_w[:, WO // 2:WO].bitcast(bf16), down_w[:, WO:DOWN])

        ident = sb("ident", [128, 128])
        identb = sb("identb", [128, 128], bf16)
        tri = sb("tri", [128, 128], bf16)
        ones_b = sb("ones_b", [128, 128], bf16)
        zero_f = sb("zero_f", [128, 2, D])
        iota_f = sb("iota_f", [128, 256])
        cst = sb("cst", [128, 128 + 128 + 256 + 128 + 1 + NC + 2 * B])
        mean_w = sb("mean_w", [128, 1])
        diag = sb("diag", [128, 2, KG, KG])
        ids_i = sb("ids_i", [128, 1 + GRAPHS, B], i32)
        idx = sb("idx", [128, 2, Q * (1 + GRAPHS)], i32)
        wp0 = sb("wp0", [128, D])
        wp1 = sb("wp1", [PG, D])
        posb = sb("posb", [128, D])
        scale_shift = sb("scale_shift", [128, 2 * D])
        gamma, beta = scale_shift[:, 0:D], scale_shift[:, D:2 * D]
        wg = sb("wg", [128, 2, GRAPHS, GRAPHS * GD])
        gbias = sb("gbias", [128, 1])
        wr = sb("wr", [128, 3 * E])
        wr0, wr1 = wr[:, 0:E], wr[:, E:3 * E]
        junk = sb("junk", [128, 1])
        filt = sb("filt", [128, 2, 4])
        net = sb("net", [16, 16 + D + 3 + 16 + S])
        w2T, w3T, net_cols = net[:, 0:16], net[:, 16:16 + D], net[:, 16 + D:19 + D]
        w1T, net_z = net[0:3, 19 + D:35 + D], net[0:3, 35 + D:35 + D + S]
        kT = sb("kT", [128, 2, NFFT])

        emb_g = sb("emb_g", [128, 2, Q, D])
        ev_g = sb("ev_g", [128, 2, GRAPHS, Q, D])
        adj_s = sb("adj_s", [128, 2, GRAPHS, Q, 128])
        grow_s = sb("grow_s", [KG, D])
        gt_s = sb("gt_s", [128, 2, KG])
        xt0 = sb("xt0", [128, 2, Q * 128])
        xt1 = sb("xt1", [128, 2, Q * 128])
        ys = sb("ys", [128, 2, Q, D])
        start = ys[:, :, :, :].rearrange("p a b d -> p (a b d)")
        pos, bproj = start[:, 0:D], start[:, D:2 * D]
        posT0, posT1 = start[:, 2 * D:2 * D + 128], start[0:D1, 2 * D + 128:2 * D + 256]
        dec = start[:, 2 * D + 256:2 * D + 512].rearrange("p (c t) -> p c t", c=2)
        sinb = start[0:16, 2 * D + 512:2 * D + 1152].rearrange("p (n t) -> p n t", n=5)
        stats = sb("stats", [128, GRP, 6])
        mv = sb("mv", [128, GRP, 2])
        rs = sb("rs", [128, 3, GRP])
        ln1 = sb("ln1", [128, Q])
        ln2 = sb("ln2", [128, 2, 2, Q])
        ln3 = sb("ln3", [128, 2, B])

        Hs = sb("Hs", [128, B, D])
        U_room = sb("U", [128, max(D * B, B * XROW // 2)])
        U = U_room[:, 0:D * B]
        Ut = U.rearrange("p (c b) -> p c b", b=B)

        wst = sb("wst", [128, WE])
        blob = sb("blob", [128, BLOB])

        xrow_f = U_room[:, 0:B * XROW // 2].rearrange("p (b x) -> p b x", b=B)
        xrow = U_room[:, 0:B * XROW // 2].bitcast(bf16).rearrange("p (b x) -> p b x", b=B)
        old_adj = adj_s[:, :, :, :, :].rearrange("p a j q h -> p (a j q h)")
        xn1 = old_adj[:, 3 * Q * 128:4 * Q * 128].rearrange("p (a n) -> p a n", a=2)
        xnT0 = old_adj[:, 0:2 * Q * 128].rearrange("p (a n) -> p a n", a=2)
        xnT1 = old_adj[:, 2 * Q * 128:3 * Q * 128].rearrange("p (a n) -> p a n", a=2)
        top = sb("top", [128, 2, Q, E])
        topi = sb("topi", [128, GRP, E], u32)
        wsm = sb("wsm", [128, 4, B])
        e01 = sb("e01", [128, 2, B])

        rt = ev_g[:, :, :, :, :].rearrange("p a g q d -> p (a g q d)")
        toep = rt[:, 0:RING * CC * 128].rearrange("p (a c t) -> p a c t", a=RING, c=CC)
        at = [0]

        def carve(n):
            at[0] += n
            assert at[0] <= 2 * GRAPHS * Q * D
            return rt[:, at[0] - n:at[0]]

        xn = carve(2 * Q * D).rearrange("p (a q d) -> p a q d", a=2, q=Q)
        oh = [carve(E * B).rearrange("p (e b) -> p e b", e=E) for _ in range(2)]
        sl = carve(E * B).rearrange("p (e b) -> p e b", e=E)
        run = carve(E * B).rearrange("p (e b) -> p e b", e=E)
        onesf = carve(B)
        ohb = sb("ohb", [128, E, B], bf16)
        cnt = carve(4 * E).rearrange("p (a e) -> p a e", a=4)
        slot = carve(2 * B).rearrange("p (b k) -> p b k", k=2)
        slq = carve(2 * B).rearrange("p (b k) -> p b k", k=2)
        slp = carve(2 * B).rearrange("p (b k) -> p b k", k=2)
        sloti = sb("sloti", [128, 3, B, 2], i32)
        cnti = sb("cnti", [128, 2, E], i32)
        row_k = sb("row_k", [128, NC])
        row_o = carve(NC)
        row_v = carve(2 * B).rearrange("p (b k) -> p b k", k=2)
        id_f = carve(NC)
        id_g = sb("id_g", [128, NC], i32)
        id_s = sb("id_s", [128, NC], i32)
        eidf = old_adj[:, 4 * Q * 128:4 * Q * 128 + NT * E].rearrange("p (t e) -> p t e", e=E)
        eidr = carve(NT)
        eid = sb("eid", [1, NT], i32)
        tp = old_adj[:, 0:2 * CC * 128].rearrange("p (a c t) -> p a c t", a=2, c=CC)
        hot_p = wst[:, 0:2 * PICKS * 128].rearrange("p (a r n) -> p a r n", a=2, r=PICKS)
        hot_q = old_adj[:, 0:2 * PICKS * NC].rearrange("p (a r n) -> p a r n", a=2, r=PICKS)
        hot_1 = blob[:, 0:2 * PICKS * 128].rearrange("p (a r n) -> p a r n", a=2, r=PICKS)

        wbuf = [U_room[:, w * BLOB:(w + 1) * BLOB] for w in range(W3)]
        flat = Hs[:, :, :].rearrange("p b d -> p (b d)")
        at_h = [0]

        def carve_h(n):
            at_h[0] += n
            assert at_h[0] <= D * B
            return flat[:, at_h[0] - n:at_h[0]]

        hf = [carve_h(FC * TS).rearrange("p (f n) -> p f n", f=FC) for _ in range(W3)]
        hh = [carve_h(FC * TS // 2).bitcast(bf16).rearrange("p (f n) -> p f n", f=FC) for _ in range(W3)]
        hl = [carve_h(FC * TS // 2).bitcast(bf16).rearrange("p (f n) -> p f n", f=FC) for _ in range(W3)]
        yo = carve_h(W3 * 2 * D).rearrange("p (a h d) -> p a h d", a=W3, h=2)
        xg_f = blob[:, 0:W3 * XROW].rearrange("p (a h x) -> p a h x", a=W3, h=2)
        xg = blob[:, 0:W3 * XROW].bitcast(bf16).rearrange("p (a h x) -> p a h x", a=W3, h=2)
        xgT = blob[:, 1200:1200 + W3 * 3 * TS // 2].bitcast(bf16).rearrange("p (a c n) -> p a c n", a=W3, c=3)
        gi = sb("gi", [128, W3, 2], i32)
        si = sb("si", [128, W3, 2], i32)
        wk = sb("wk", [128, W3, 2])

        bank = [ctx.enter_context(nc.psum_tensor(f"bank{i}", [128, 512], fp32)) for i in range(8)]

        loaded = sem("loaded")
        ids_in = sem("ids_in")
        cast_done = sem("cast_done")
        filt_step = sem("filt_step")
        filt_in = sem("filt_in")
        filt_arg = sem("filt_arg")
        kpad_stored = sem("kpad_stored")
        kready = sem("kready")
        dec_done = sem("dec_done")
        pos_done = sem("pos_done")
        pos_t = sem("pos_t")
        pos_ts = sem("pos_ts")
        adj_in = [sem(f"adj_in{p}") for p in range(2)]
        idx_staged = sem("idx_staged")
        emb_in = [sem(f"emb_in{p}") for p in range(2)]
        ev_in = [sem(f"ev_in{p}") for p in range(2)]
        pool_turn = sem("pool_turn")
        pe_turn = sem("pe_turn")
        sp_turn = sem("sp_turn")
        colsum = sem("colsum")
        diag_ready = sem("diag_ready")
        emb_t = sem("emb_t")
        xt_ready = sem("xt_ready")
        gvec = sem("gvec")
        grow_ready = sem("grow_ready")
        gt = sem("gt")
        gt_ready = sem("gt_ready")
        gfeat = sem("gfeat")
        gfeat_ready = sem("gfeat_ready")
        proj = sem("proj")
        proj_read = sem("proj_read")
        ln_ready = sem("ln_ready")
        rows_done = sem("rows_done")
        moments_done = sem("moments_done")
        w_in = sem("w_in")
        w_hi = sem("w_hi")
        w_lo = sem("w_lo")
        w_out = sem("w_out")
        toep_in = [sem(f"toep_in{s}") for s in range(RING)]
        turned = sem("turned")
        conv = sem("conv")
        conv_read = sem("conv_read")
        ln_done = sem("ln_done")
        hi_done = sem("hi_done")
        lo_done = sem("lo_done")
        xrow_out = sem("xrow_out")
        h_out = sem("h_out")
        xn_t = sem("xn_t")
        xn1_ready = sem("xn1_ready")
        xnT_ready = sem("xnT_ready")
        logits = sem("logits")
        gap_ready = sem("gap_ready")
        exp_done = sem("exp_done")
        wts_done = sem("wts_done")
        hot_ready = sem("hot_ready")
        ranks = sem("ranks")
        eid_done = sem("eid_done")
        hot_1_ready = sem("hot_1_ready")
        hot_p_ready = sem("hot_p_ready")
        hot_q_ready = sem("hot_q_ready")
        pick_used = sem("pick_used")
        table = sem("table")
        ids_done = sem("ids_done")
        wi_in = [sem(f"wi_in{w}") for w in range(W3)]
        wo_in = [sem(f"wo_in{w}") for w in range(W3)]
        stage_done = sem("stage_done")
        xg_in = [sem(f"xg_in{w}") for w in range(W3)]
        xg_t = sem("xg_t")
        xgT_ready = sem("xgT_ready")
        up = sem("up")
        gelu = sem("gelu")
        hid = sem("hid")
        down = sem("down")
        biased = sem("biased")
        yo_ready = sem("yo_ready")
        scat = [sem(f"scat{h}") for h in range(2)]

        block = ctx.enter_context(nc.Block())

        N_LOADS = 16

        def store_expert(eng, e):
            eng.wait_ge(w_lo, e + 1)
            eng.dma_start(blob_d[bass.ds(e, 1), :, :].rearrange("e p x -> p (e x)"), blob[:, :]).then_inc(w_out, 16)

        @block.sync
        def _(sp):
            n = [0]

            def load(dst, src):
                n[0] += 1
                sp.dma_start(dst, src).then_inc(loaded, 16)

            sp.dma_start(ids_i[:, :, :], t["ids"].rearrange("p (j b) -> p j b", j=1 + GRAPHS)).then_inc(ids_in, 16)
            load(cst[:, :], t["cst"])
            load(wp0[:, :], t["WpT"][0:D0, :])
            load(wp1[:, :], t["WpT"][D0:D0 + PG, :])
            load(pos[:, :], t["pos"])
            load(bproj[:, :], t["b_proj"].partition_broadcast(128))
            load(scale_shift[:, :], t["gamma_beta"].partition_broadcast(128))
            for c, rows in ((0, D0), (1, D1)):
                own = bass.AP(tensor=wg, offset=c * GRAPHS * GRAPHS * GD,
                              ap=[[2 * GRAPHS * GRAPHS * GD, rows], [(GRAPHS + 1) * GD, GRAPHS], [1, GD]])
                load(own, t["WgT"][c * D0:c * D0 + rows, :].rearrange("d (j g) -> d j g", j=GRAPHS))
            load(gbias[D1:PG, :], t["gbias"])
            load(wr0, t["WrT"][0:D0, :])
            for h in range(2):
                load(wr1[h * D1:(h + 1) * D1, h * E:(h + 1) * E], t["WrT"][D0:D, :])
            load(filt[:, 0, 0:3], t["filt"][0:D0, :])
            load(filt[0:D1, 1, 0:3], t["filt"][D0:D, :])
            load(net[:, 0:19 + D], t["net"])
            load(net[0:3, 19 + D:35 + D + S], t["net_in"])
            assert n[0] == N_LOADS, n[0]

            def load_adj(i, p):
                for j in range(GRAPHS):
                    sp.dma_start(adj_s[:, p, j, :, :],
                                 t["adj"][j][bass.ds(i * Q, Q), :, :].rearrange("b g h -> g b h")).then_inc(adj_in[p], 16)

            def load_expert(e):
                sp.dma_start(wst[:, :], t["wsrc"][bass.ds(e, 1), :, :].rearrange("e p x -> p (e x)")).then_inc(w_in, 16)
                bi, bo = parts(blob)[2], parts(blob)[5]
                sp.dma_start(bi, t["bi"][bass.ds(e, 1), :, :].rearrange("e p x -> p (e x)")).then_inc(w_in, 16)
                sp.dma_start(bo,
                              t["bo"][bass.ds(e, 1), :, :].rearrange("e o x -> o (e x)").to_broadcast([128, D])).then_inc(w_in, 16)

            load_adj(0, 0)
            load_adj(1, 1)
            load_expert(0)
            with sp.Fori(0, NQ // 2 - 1) as it:
                for p in range(2):
                    sp.wait_ge(colsum, 2 * it + p + 1)
                    load_adj(2 * it + p + 2, p)
                sp.wait_ge(w_out, 16 * (it + 1))
                sp.sem_inc(sp_turn, 1)
                load_expert(it + 1)

            sp.wait_ge(kready, 2)
            sp.dma_start(kpad_d[0:D0, :], kT[:, 0, :]).then_inc(kpad_stored, 16)
            sp.dma_start(kpad_d[D0:D, :], kT[0:D1, 1, :]).then_inc(kpad_stored, 16)
            sp.wait_ge(kpad_stored, 32)

            def load_toep(c, s):
                src = bass.AP(tensor=kpad_d.tensor, offset=c * (CC * NFFT), ap=[[1, 128], [NFFT, CC], [1, 128]])
                sp.dma_start(toep[:, s, :, :], src).then_inc(toep_in[s], 16)

            sp.wait_ge(gvec, NQ)
            for s in range(RING):
                load_toep(s, s)
            store_expert(sp, E - 1)
            with sp.Fori(1, NCH // RING) as it:
                for s in range(RING):
                    sp.wait_ge(turned, it * RING + s + 1 - RING)
                    load_toep(it * RING + s, s)

            def store_rows(g):
                sp.dma_start(out_rows[bass.ds(g * GRP, GRP), :, :].rearrange("b s d -> s b d"),
                             Hs[:, bass.ds(g * GRP, GRP), :]).then_inc(h_out, 16)
                sp.wait_ge(wts_done, g + 1)
                sp.sem_inc(sp_turn, 1)
                sp.wait_ge(lo_done, QG * (g + 1))
                sp.sem_inc(sp_turn, 1)
                sp.dma_start(xtab_d[bass.ds(g * (GRP * S), GRP * S), :].rearrange("(b s) x -> s b x", s=S),
                             xrow_f[:, bass.ds(g * GRP, GRP), :]).then_inc(xrow_out, 16)

            sp.wait_ge(cast_done, 1)
            sp.dma_start(out[B * S:B * S + SPARE, :].rearrange("(a p) d -> p a d", a=2),
                         zero_f[:, :, :]).then_inc(h_out, 16)
            sp.wait_ge(conv_read, NCH)
            with sp.Fori(0, NG) as g:
                store_rows(g)

            sp.wait_ge(w_out, 16 * E)
            sp.wait_ge(xrow_out, 16 * NG)
            sp.wait_ge(eid_done, 1)

            def expert(q):
                return sp.value_load(eid[0:1, bass.ds(q, 1)], min_val=0, max_val=E - 1)

            def load_up(e, w):
                sp.dma_start(wbuf[w][:, 0:UP], blob_d[bass.ds(e, 1), :, 0:UP].rearrange("e p x -> p (e x)")).then_inc(wi_in[w], 16)

            def load_down(e, w):
                sp.dma_start(wbuf[w][:, UP:BLOB], blob_d[bass.ds(e, 1), :, UP:BLOB].rearrange("e p x -> p (e x)")).then_inc(wo_in[w], 16)

            for w in range(W3):
                load_up(expert(w), w)
                load_down(expert(w), w)

            def reload(it):
                for w in range(W3):
                    q = W3 * it + w
                    if isinstance(q, int) and q >= NT:
                        break
                    e, held = expert(q), expert(q - W3)
                    sp.wait_ge(gelu, FC // 2 * (q - W3 + 1))
                    sp.sem_inc(sp_turn, 1)
                    with sp.If(e != held):
                        load_up(e, w)
                    with sp.Else():
                        sp.sem_inc(wi_in[w], 16)
                    sp.wait_ge(biased, q - W3 + 1)
                    sp.sem_inc(sp_turn, 1)
                    with sp.If(e != held):
                        load_down(e, w)
                    with sp.Else():
                        sp.sem_inc(wo_in[w], 16)

            with sp.Fori(1, ROUNDS - 1) as it:
                reload(it)
            reload(ROUNDS - 1)
            sp.wait_ge(h_out, 16 * (NG + 1))
            for h in range(2):
                sp.wait_ge(scat[h], 16 * NT)

        @block.gpsimd
        def _(pool):
            def gathers(i, p):
                if not (isinstance(i, int) and i < 2):
                    pool.wait_ge(gvec, i - 1)
                nc.gpsimd.tensor_copy(idx[:, p, :].rearrange("p (j b) -> p j b", b=Q), ids_i[:, :, bass.ds(i * Q, Q)]).then_inc(idx_staged, 1)
                pool.wait_ge(idx_staged, i + 1)
                pool.sem_inc(pool_turn, 1)
                for b in range(Q):
                    pool.indirect_dma_start(emb_g[:, p, b, :], None, t["word_emb"],
                                            bass.IndirectOffsetOnAxis(ap=idx[:, p, b:b + 1], axis=0)).then_inc(emb_in[p], 16)
                for j in range(GRAPHS):
                    for b in range(Q):
                        k = (1 + j) * Q + b
                        pool.indirect_dma_start(ev_g[:, p, j, b, :], None, t["word_emb"],
                                                bass.IndirectOffsetOnAxis(ap=idx[:, p, k:k + 1], axis=0)).then_inc(ev_in[p], 16)

            pool.wait_ge(ids_in, 16)
            gathers(0, 0)
            gathers(1, 1)
            with pool.Fori(1, NQ // 2) as it:
                for p in range(2):
                    gathers(2 * it + p, p)

            def low(i, p):
                pool.wait_ge(ln_done, i + 1)
                after(pool, xn_t, i - 1)
                pool.sem_inc(pool_turn, 1)
                nc.gpsimd.tensor_copy(xn1[:, p, :].rearrange("p (b d) -> p b d", b=Q), xn[:, p, :, D0:D]).then_inc(xn1_ready, 1)
                pool.wait_ge(hi_done, i + 1)
                b = bass.ds(i * Q, Q)
                nc.gpsimd.tensor_tensor(xrow[:, b, D:D + D1], xn[:, p, :, D0:D], xrow[:, b, D0:D], ALU.subtract)
                nc.gpsimd.tensor_tensor(xrow[:, b, D + D1:2 * D], xn[:, p, :, 0:D0], xrow[:, b, 0:D0], ALU.subtract).then_inc(lo_done, 1)

            def lows(it):
                for p in range(2):
                    low(2 * it + p, p)

            steps(pool, NQ // 2, lows)

            def fetch(q, w):
                pool.wait_ge(stage_done, q + 1)
                pool.sem_inc(pool_turn, 1)
                for h in range(2):
                    pool.indirect_dma_start(xg_f[:, w, h, :], None, xtab_d,
                                            bass.IndirectOffsetOnAxis(ap=gi[:, w, h:h + 1], axis=0)).then_inc(xg_in[w], 16)

            def add_rows(q, p):
                for h in range(2):
                    after(pool, scat[h], 16 * q)
                pool.wait_ge(yo_ready, q + 1)
                pool.sem_inc(pool_turn, 1)
                for h in range(2):
                    pool.indirect_dma_start(out, bass.IndirectOffsetOnAxis(ap=si[:, p, h:h + 1], axis=0), yo[:, p, h, :], None,
                                            compute_op=ALU.add).then_inc(scat[h], 16)

            pool.wait_ge(xrow_out, 16 * NG)
            pool.wait_ge(hot_p_ready, 2 * B // PICKS)
            fetch(0, 0)
            fetch(1, 1)
            pool.wait_ge(h_out, 16 * (NG + 1))

            def tiles(it):
                for w in range(W3):
                    q = W3 * it + w
                    if isinstance(q, int) and q >= NT:
                        break
                    if not (isinstance(q, int) and q + 2 >= NT):
                        fetch(q + 2, (w + 2) % W3)
                    if not (isinstance(q, int) and q < 2):
                        add_rows(q - 2, (w + 1) % W3)

            steps(pool, ROUNDS, tiles, last=1)
            for q in range(NT - 2, NT):
                add_rows(q, q % W3)

        @block.tensor
        def _(pe):
            mm = nc.tensor.matmul
            pe.wait_ge(loaded, 16 * N_LOADS)
            mm(bank[0][0:16, 0:128], w1T, net_z, start=True, stop=True).then_inc(filt_step, 1)
            nc.tensor.transpose(bank[1][:, 0:128], pos[:, 0:D0], cst[:, 0:128])
            nc.tensor.transpose(bank[1][0:D1, 128:256], pos[:, D0:D], cst[:, 0:128]).then_inc(pos_t, 1)
            pe.wait_ge(pos_ts, 1)
            mm(bank[2][:, 0:D], posT0[:, :], wp0[:, :], start=True, stop=False)
            mm(bank[2][:, 0:D], posT1[:, :], wp1[0:D1, :], start=False, stop=True).then_inc(pos_t, 1)
            pe.wait_ge(filt_in, 1)
            mm(bank[0][0:16, 128:256], w2T, sinb[:, 3, :], start=True, stop=True).then_inc(filt_step, 1)
            pe.wait_ge(filt_in, 2)
            mm(bank[0][:, 256:384], w3T[:, 0:D0], sinb[:, 4, :], start=True, stop=True)
            mm(bank[0][0:D1, 384:512], w3T[:, D0:D], sinb[:, 4, :], start=True, stop=True).then_inc(filt_step, 1)
            pe.wait_ge(kready, 2)
            pe.wait_ge(pos_done, 1)
            pe.wait_ge(cast_done, 1)

            def quad(it, p):
                i = 2 * it + p
                pe.wait_ge(adj_in[p], 16 * GRAPHS * (it + 1))
                for j in range(GRAPHS):
                    for b in range(Q):
                        k = p * KG + j * Q + b
                        last = mm(bank[0][:, k:k + 1], adj_s[:, p, j, b, :], mean_w[:, :], start=True, stop=True)
                last.then_inc(colsum, 1)
                after(pe, xt_ready, i)
                pe.wait_ge(emb_in[p], 16 * Q * (it + 1))
                for b in range(Q):
                    nc.tensor.transpose(bank[1][:, b * 128:(b + 1) * 128], emb_g[:, p, b, 0:D0], ident[:, :])
                    last = nc.tensor.transpose(bank[2][0:D1, b * 128:(b + 1) * 128], emb_g[:, p, b, D0:D], ident[:, :])
                last.then_inc(emb_t, 1)
                pe.wait_ge(diag_ready, i + 1)
                pe.wait_ge(ev_in[p], 16 * KG * (it + 1))
                for j in range(GRAPHS):
                    for b in range(Q):
                        k = j * Q + b
                        last = mm(bank[3][0:KG, 0:D], diag[:, p, k, :], ev_g[:, p, j, b, :],
                                  start=k == 0, stop=k == KG - 1)
                last.then_inc(gvec, 1)
                pe.wait_ge(grow_ready, i + 1)
                pe.sem_inc(pe_turn, 1)
                nc.tensor.transpose(bank[0][0:D1, 64:64 + KG], grow_s[:, D0:D], ident[0:KG, 0:KG])
                nc.tensor.transpose(bank[0][:, 32:32 + KG], grow_s[:, 0:D0], ident[0:KG, 0:KG]).then_inc(gt, 1)
                pe.wait_ge(gt_ready, i + 1)
                for j in range(GRAPHS):
                    for c, n in ((0, D0), (1, D1)):
                        last = mm(bank[3][D1:PG, 256:256 + Q], wg[0:n, c, j, :], gt_s[0:n, c, j * Q:(j + 1) * Q],
                                  start=j == 0 and c == 0, stop=j == GRAPHS - 1 and c == 1)
                last.then_inc(gfeat, 1)
                after(pe, proj_read, i - 1)
                pe.wait_ge(gfeat_ready, i + 1)
                for b in range(Q):
                    ps = bank[4 + 2 * p + b // 2][:, (b % 2) * D:(b % 2 + 1) * D]
                    mm(ps, xt0[:, p, b * 128:(b + 1) * 128], wp0[:, :], start=True, stop=False)
                    last = mm(ps, xt1[0:PG, p, b * 128:(b + 1) * 128], wp1[:, :], start=False, stop=True)
                last.then_inc(proj, 1)

            def pair(it):
                for p in range(2):
                    quad(it, p)

            steps(pe, NQ // 2, pair)

            pe.wait_ge(rows_done, NQ)

            def chunk(it, s):
                c = it * RING + s
                pe.wait_ge(turned, c + 1)
                for k in range(CC):
                    n = 2 if k < CC - 1 else 1
                    last = mm(bank[6 + s % 2][:, k * B:(k + n) * B], tp[:, s % 2, k, :],
                              Ut[:, bass.ds(c * CC + k, n), :].rearrange("p c b -> p (c b)"), start=True, stop=True)
                last.then_inc(conv, 1)

            for s in range(RING):
                if s >= 2:
                    pe.wait_ge(conv_read, s - 1)
                chunk(0, s)
            with pe.Fori(1, NCH // RING) as it:
                for s in range(RING):
                    pe.wait_ge(conv_read, it * RING + s - 1)
                    chunk(it, s)

            def turn_quad(i, p):
                pe.wait_ge(ln_done, i + 1)
                pe.wait_ge(xn1_ready, i + 1)
                after(pe, xnT_ready, i)
                for b in range(Q):
                    nc.tensor.transpose(bank[1][:, b * 128:(b + 1) * 128], xn[:, p, b, 0:D0], ident[:, :])
                for h in range(Q // 2):
                    last = nc.tensor.transpose(bank[2][:, h * 128:(h + 1) * 128], xn1[:, p, h * 128:(h + 1) * 128], ident[:, :])
                last.then_inc(xn_t, 1)

            def score(i, s):
                p = s % 2
                pe.wait_ge(xnT_ready, i + 1)
                after(pe, gap_ready, i - QG + 1)
                for h in range(Q // 2):
                    mm(bank[3 + s][:, h * 2 * E:(h + 1) * 2 * E], xnT1[:, p, h * 128:(h + 1) * 128], wr1, start=True, stop=False)
                    for b in (2 * h, 2 * h + 1):
                        last = mm(bank[3 + s][:, b * E:(b + 1) * E], xnT0[:, p, b * 128:(b + 1) * 128], wr0, start=False, stop=b % 2 == 1)
                last.then_inc(logits, 1)

            def rank(g):
                pe.wait_ge(hot_ready, g + 1)
                hot = ohb[:, :, bass.ds(g * GRP, GRP)]
                for to, w in ((7, tri), (0, ones_b)):
                    to_g = bank[to][:, :].rearrange("p (e b) -> p e b", e=E)[:, :, bass.ds(g * GRP, GRP)]
                    last = mm(to_g, w[:, :], hot, start=True, stop=True)
                last.then_inc(ranks, 1)

            turn_quad(0, 0)

            def routes(g):
                for s in range(QG):
                    i = QG * g + s
                    if not (isinstance(i, int) and i == NQ - 1):
                        turn_quad(i + 1, (s + 1) % 2)
                    score(i, s)
                    if s == QG - 1 and not (isinstance(g, int) and g == 0):
                        rank(g - 1)

            steps(pe, NG, routes, last=1)
            rank(NG - 1)

            mm(bank[6][:, 0:NC], zero_f[:, 0, 0:128], iota_f[:, 0:NC], start=True, stop=False)
            with pe.Fori(0, B // PICKS) as it:
                for a in range(2):
                    pe.wait_ge(hot_p_ready, 2 * it + a + 1)
                    pe.wait_ge(hot_q_ready, 2 * it + a + 1)
                    for r in range(PICKS):
                        last = mm(bank[6][:, 0:NC], hot_p[:, a, r, :], hot_q[:, a, r, :], start=False, stop=False)
                    last.then_inc(pick_used, 1)
            mm(bank[6][:, 0:NC], zero_f[:, 0, 0:128], iota_f[:, 0:NC], start=False, stop=True).then_inc(table, 1)
            pe.wait_ge(ids_done, 1)

            xT_ps = bank[0][:, :].bitcast(bf16)

            def turn_rows(it, w):
                pe.wait_ge(xg_in[w], 32 * (it + 1))
                for h in range(2):
                    for c in range(3):
                        last = nc.tensor.transpose(xT_ps[:, c * TS + h * 128:c * TS + h * 128 + 128],
                                                   xg[:, w, h, c * 128:(c + 1) * 128], identb[:, :])
                last.then_inc(xg_t, 1)

            def up_tile(it, w):
                q = W3 * it + w
                hi, lo = parts(wbuf[w])[0:2]
                pe.wait_ge(xgT_ready, q + 1)
                pe.wait_ge(wi_in[w], 16 * (it + 1))
                x0, x1, x2 = (xgT[:, w, c, :] for c in range(3))
                for f in range(FC):
                    if f % 2 == 0:
                        after(pe, gelu, FC // 2 * (q - 1) + f // 2 + 1)
                    ps = bank[2 + f // 2][:, (f % 2) * TS:(f % 2 + 1) * TS]
                    a = slice(f * 128, (f + 1) * 128)
                    r = slice(F + f * 128, F + (f + 1) * 128)
                    mm(ps, hi[:, a], x0, start=True, stop=False)
                    mm(ps, hi[:, a], x2, start=False, stop=False)
                    mm(ps, lo[:, a], x0, start=False, stop=False)
                    mm(ps, hi[:, r], x1, start=False, stop=False)
                    last = mm(ps, lo[0:D1, r], x1[0:D1, :], start=False, stop=True)
                    if f % 2:
                        last.then_inc(up, 1)

            def down_tile(it, w):
                q = W3 * it + w
                hi, lo = parts(wbuf[w])[3:5]
                pe.wait_ge(wo_in[w], 16 * (it + 1))
                pe.wait_ge(hid, q + 1)
                after(pe, biased, q - W3 + 1)
                for h in range(2):
                    ps = bank[5 + w][:, h * D:(h + 1) * D]
                    for f in range(FC):
                        c = slice(f * D, (f + 1) * D)
                        n = slice(h * 128, (h + 1) * 128)
                        mm(ps, hh[w][:, f, n], hi[:, c], start=f == 0, stop=False)
                        mm(ps, hh[w][:, f, n], lo[:, c], start=False, stop=False)
                        last = mm(ps, hl[w][:, f, n], hi[:, c], start=False, stop=f == FC - 1)
                last.then_inc(down, 1)

            turn_rows(0, 0)

            def tiles(it):
                for w in range(W3):
                    q = W3 * it + w
                    if isinstance(q, int) and q >= NT:
                        break
                    up_tile(it, w)
                    if not (isinstance(q, int) and q + 1 >= NT):
                        turn_rows(it + (w + 1) // W3, (w + 1) % W3)
                    if not (isinstance(q, int) and q == 0):
                        down_tile(it if w else it - 1, (w - 1) % W3)

            steps(pe, ROUNDS, tiles, last=1)
            down_tile((NT - 1) // W3, (NT - 1) % W3)

        @block.scalar
        def _(act):
            f = nc.scalar.activation
            act.wait_ge(pos_t, 1)
            f(posT0[:, :], bank[1][:, 0:128], ACT.Copy)
            f(posT1[:, :], bank[1][0:D1, 128:256], ACT.Copy).then_inc(pos_ts, 1)
            for n in range(2):
                act.wait_ge(filt_arg, n + 1)
                f(sinb[:, 3 + n, :], sinb[:, 2, :], ACT.Sin).then_inc(filt_in, 1)
            act.wait_ge(cast_done, 1)
            act.wait_ge(loaded, 16 * N_LOADS)
            trow = cst[:, 512:640]
            f(dec[:, 0, :], trow, ACT.Exp, scale=filt[:, 0, 3:4])
            f(dec[0:D1, 1, :], trow[0:D1, :], ACT.Exp, scale=filt[0:D1, 1, 3:4]).then_inc(dec_done, 1)

            def quad(it, p):
                i = 2 * it + p
                act.wait_ge(colsum, i + 1)
                on_diag = bass.AP(tensor=diag, offset=p * KG * KG, ap=[[2 * KG * KG, 128], [KG + 1, KG]])
                f(on_diag, bank[0][:, p * KG:(p + 1) * KG], ACT.Copy).then_inc(diag_ready, 1)
                act.wait_ge(emb_t, i + 1)
                after(act, proj, i - 1)
                f(xt0[:, p, :], bank[1][:, :], ACT.Copy)
                f(xt1[0:D1, p, :], bank[2][0:D1, :], ACT.Copy).then_inc(xt_ready, 1)

            def graphs(it, p):
                i = 2 * it + p
                act.wait_ge(gvec, i + 1)
                f(grow_s[:, :], bank[3][0:KG, 0:D], ACT.Copy).then_inc(grow_ready, 1)
                act.wait_ge(gt, i + 1)
                f(gt_s[:, 0, :], bank[0][:, 32:32 + KG], ACT.Copy)
                f(gt_s[0:D1, 1, :], bank[0][0:D1, 64:64 + KG], ACT.Copy).then_inc(gt_ready, 1)
                act.wait_ge(gfeat, i + 1)
                f(xt1[D1:PG, p, :].rearrange("p (b s) -> p b s", b=Q), repeat(bank[3][D1:PG, 256:256 + Q], 2, 128), ACT.Relu,
                  bias=gbias[D1:PG, :]).then_inc(gfeat_ready, 1)

            def normal(i, p):
                act.wait_ge(ln_ready, i + 1)
                for b in range(Q):
                    last = f(Ut[:, :, bass.ds(i * Q + b, 1)].rearrange("p c b -> p (c b)"),
                             Hs[:, bass.ds(i * Q + b, 1), :].rearrange("p b d -> p (b d)"), ACT.Identity,
                             scale=ln2[:, p, 0, b:b + 1], bias=ln2[:, p, 1, b:b + 1])
                last.then_inc(rows_done, 1)

            def split_hi(e):
                act.wait_ge(w_in, 48 * (e + 1))
                f(parts(blob)[0], wst[:, 0:WI], ACT.Copy)
                f(parts(blob)[3], wst[:, WI:WE], ACT.Copy).then_inc(w_hi, 1)

            def pairs(it):
                quad(it, 0)
                graphs(it, 0)
                if not (isinstance(it, int) and it == 0):
                    normal(2 * it - 1, 1)
                quad(it, 1)
                split_hi(it)
                graphs(it, 1)
                normal(2 * it, 0)
                if not (isinstance(it, int) and it > 0):
                    store_expert(act, it)

            steps(act, NQ // 2, pairs, last=1)

            def turn(it, s):
                act.wait_ge(toep_in[s], 16 * (it + 1))
                after(act, conv, it * RING + s - 1)
                f(tp[:, s % 2, :, :], reverse(toep[:, s, :, :]), ACT.Copy).then_inc(turned, 1)

            turn(0, 0)
            turn(0, 1)
            normal(NQ - 1, 1)
            for s in range(2, RING):
                turn(0, s)
            with act.Fori(1, NCH // RING) as it:
                for s in range(RING):
                    turn(it, s)

            def row_parts(i, p):
                after(act, xn_t, i - 1)
                after(act, lo_done, i - 1)
                for b in range(Q):
                    last = f(xn[:, p, b, :], Hs[:, bass.ds(i * Q + b, 1), :].rearrange("p b d -> p (b d)"), ACT.Identity,
                             scale=ln3[:, 0, bass.ds(i * Q + b, 1)], bias=ln3[:, 1, bass.ds(i * Q + b, 1)])
                last.then_inc(ln_done, 1)
                act.wait_ge(ln_done, i + 1)
                f(xrow[:, bass.ds(i * Q, Q), 0:D], xn[:, p, :, :], ACT.Copy).then_inc(hi_done, 1)

            def turned_parts(i, p):
                act.wait_ge(xn_t, i + 1)
                after(act, logits, i - 1)
                f(xnT0[:, p, :], bank[1][:, :], ACT.Copy)
                f(xnT1[:, p, :], bank[2][:, 0:2 * 128], ACT.Copy).then_inc(xnT_ready, 1)

            def gap_exp(g):
                act.wait_ge(gap_ready, QG * (g + 1))
                f(wsm[:, 1, bass.ds(g * GRP, GRP)], wsm[:, 0, bass.ds(g * GRP, GRP)], ACT.Exp).then_inc(exp_done, 1)

            act.wait_ge(moments_done, 1)
            row_parts(0, 0)

            def groups(g):
                for s in range(QG):
                    i = QG * g + s
                    if not (isinstance(i, int) and i == NQ - 1):
                        if s == 1 and isinstance(g, int) and g == 0:
                            act.wait_ge(moments_done, 2)
                        if s == QG - 1:
                            act.wait_ge(moments_done, g + 3)
                        row_parts(i + 1, (s + 1) % 2)
                    turned_parts(i, s % 2)
                    if s == 2 and not (isinstance(g, int) and g == 0):
                        gap_exp(g - 1)

            steps(act, NG, groups, last=1)
            gap_exp(NG - 1)
            f(junk[:, :], mean_w[:, :], ACT.Gelu)

            def hots(it):
                for a in range(2):
                    n = 2 * it + a
                    act.wait_ge(hot_1_ready, n + 1)
                    after(act, pick_used, n - 1)
                    for r in range(PICKS):
                        b, k = bass.ds(n * (PICKS // 2) + r // 2, 1), r % 2
                        last = f(hot_p[:, a, r, :], hot_1[:, a, r, :], ACT.Copy, scale=row_v[:, b, k])
                    last.then_inc(hot_p_ready, 1)

            steps(act, B // PICKS, hots)
            act.wait_ge(h_out, 16 * (NG + 1))

            def hidden(q, w):
                bi = parts(wbuf[w])[2]
                for c in range(0, FC, 2):
                    act.wait_ge(up, FC // 2 * q + c // 2 + 1)
                    for d in (c, c + 1):
                        ps = bank[2 + c // 2][:, (d % 2) * TS:(d % 2 + 1) * TS]
                        f(hh[w][:, d, :], ps, ACT.Gelu, bias=bi[:, d:d + 1])
                        last = f(hf[w][:, d, :], ps, ACT.Gelu, bias=bi[:, d:d + 1])
                    last.then_inc(gelu, 1)

            def tiles(it):
                for w in range(W3):
                    q = W3 * it + w
                    if isinstance(q, int) and q >= NT:
                        break
                    after(act, down, q - W3 + 1)
                    hidden(q, w)

            steps(act, ROUNDS, tiles, last=1)

        @block.vector
        def _(dve):
            v = nc.vector
            fence = dve.drain

            dve.wait_ge(loaded, 16 * N_LOADS)
            v.tensor_copy(ident[:, :], cst[:, 0:128])
            v.tensor_copy(identb[:, :], cst[:, 0:128])
            v.tensor_copy(tri[:, :], cst[:, 128:256])
            v.tensor_copy(iota_f[:, :], cst[:, 256:512])
            v.memset(diag[:, :, :, :], 0.0)
            v.memset(ones_b[:, :], 1.0)
            v.memset(zero_f[:, :, :], 0.0)
            v.memset(mean_w[:, :], 1.0 / 128)
            for h in range(2):
                v.memset(wr1[h * D1:(h + 1) * D1, (1 - h) * E:(2 - h) * E], 0.0)
            v.memset(kT[:, :, S:NFFT], 0.0)
            for j in range(GRAPHS):
                for k in range(GRAPHS):
                    if k != j:
                        v.memset(wg[:, :, j, k * GD:(k + 1) * GD], 0.0)
            v.tensor_scalar(filt[:, 0, 3:4], filt[:, 0, 0:1], -1.0, None, ALU.mult)
            v.tensor_scalar(filt[0:D1, 1, 3:4], filt[0:D1, 1, 0:1], -1.0, None, ALU.mult).then_inc(cast_done, 1)

            for n in range(2):
                dve.wait_ge(filt_step, n + 1)
                fence()
                v.tensor_scalar(sinb[:, 0, :], bank[0][0:16, n * 128:(n + 1) * 128], net_cols[:, n:n + 1], net_cols[:, 2:3], ALU.add, ALU.mult)
                fence()
                v.tensor_scalar(sinb[:, 1, :], sinb[:, 0, :], 1.0 / TWO_PI, MAGIC, ALU.mult, ALU.add)
                fence()
                v.tensor_scalar(sinb[:, 1, :], sinb[:, 1, :], MAGIC, None, ALU.subtract)
                src = sinb[:, 0, :]
                if n:
                    dve.wait_ge(filt_in, n)
                for c in (C1, C2, C3):
                    fence()
                    v.scalar_tensor_tensor(sinb[:, 2, :], sinb[:, 1, :], -c, src, ALU.mult, ALU.add)
                    src = sinb[:, 2, :]
                fence()
                v.tensor_scalar(sinb[:, 2, :], sinb[:, 2, :], 3.1415925, -3.1415925, ALU.min, ALU.max).then_inc(filt_arg, 1)
            dve.wait_ge(filt_step, 3)
            dve.wait_ge(dec_done, 1)
            for c, n in ((0, D0), (1, D1)):
                kk = kT[0:n, c, 0:S]
                v.tensor_scalar(kk, bank[0][0:n, 256 + 128 * c:384 + 128 * c], filt[0:n, c, 1:2], 1.0 / NFFT, ALU.add, ALU.mult)
                fence()
                v.tensor_tensor(kk, kk, dec[0:n, c, :], ALU.mult)
                fence()
                v.tensor_tensor(kT[0:n, c, S - 1:S], kT[0:n, c, S - 1:S], filt[0:n, c, 2:3], ALU.add).then_inc(kready, 1)
            dve.wait_ge(pos_t, 2)
            v.tensor_tensor(posb[:, :], bank[2][:, 0:D], bproj[:, :], ALU.add).then_inc(pos_done, 1)

            def rsqrt(n, out_ap, eps):
                y, t, x = rs[:, 0, 0:n], rs[:, 1, 0:n], rs[:, 2, 0:n]
                v.tensor_scalar(x, mv[:, 0:n, 1], eps, None, ALU.add)
                fence()
                v.tensor_scalar(y.bitcast(i32), x.bitcast(i32), 1, None, ALU.logical_shift_right)
                v.tensor_scalar(x, x, -0.5, None, ALU.mult)
                fence()
                v.tensor_scalar(y.bitcast(i32), y.bitcast(i32), -1.0, float(0x5F3759DF), ALU.mult, ALU.add)
                for step in range(3):
                    fence()
                    v.tensor_tensor(t, y, y, ALU.mult)
                    fence()
                    v.tensor_tensor(t, t, x, ALU.mult)
                    fence()
                    v.scalar_tensor_tensor(out_ap if step == 2 else y, t, 1.5, y, ALU.add, ALU.mult)
                fence()

            def aggregate(n):
                fence()
                for b in range(n):
                    v.bn_aggr(mv[:, b, :], stats[:, b, :])
                fence()

            def moments(n, src):
                for b in range(n):
                    v.bn_stats(stats[:, b, :], src(b))
                aggregate(n)

            def rows(i, p):
                dve.wait_ge(proj, i + 1)
                for h in range(Q // 2):
                    last = v.tensor_tensor(ys[:, p, 2 * h:2 * h + 2, :], bank[4 + 2 * p + h][:, 0:2 * D].rearrange("p (b d) -> p b d", b=2),
                                           repeat(posb[:, :], 1, 2), ALU.add)
                last.then_inc(proj_read, 1)
                fence()
                moments(Q, lambda b: ys[:, p, b, :])
                rsqrt(Q, ln1[:, :], EPS_TOK)
                h = lambda b: Hs[:, bass.ds(i * Q + b, 1), :].rearrange("p b d -> p (b d)")
                for b in range(Q):
                    v.scalar_tensor_tensor(ys[:, p, b, :], ys[:, p, b, :], mv[:, b, 0:1], gamma[:, :], ALU.subtract, ALU.mult)
                fence()
                for b in range(Q):
                    v.scalar_tensor_tensor(h(b), ys[:, p, b, :], ln1[:, b:b + 1], beta[:, :], ALU.mult, ALU.add)
                fence()
                moments(Q, h)
                after(dve, rows_done, i - 1)
                rsqrt(Q, ln2[:, p, 0, :], EPS_LN)
                v.scalar_tensor_tensor(ln2[:, p, 1, :], mv[:, 0:Q, 0], -1.0, ln2[:, p, 0, :], ALU.mult, ALU.mult).then_inc(ln_ready, 1)
                fence()

            def split_lo(e):
                dve.wait_ge(w_hi, e + 1)
                hi_up, lo_up, _, hi_down, lo_down, _ = parts(blob)
                v.tensor_tensor(lo_up, wst[:, 0:WI], hi_up, ALU.subtract)
                v.tensor_tensor(lo_down, wst[:, WI:WE], hi_down, ALU.subtract).then_inc(w_lo, 1)

            def pairs(it):
                rows(2 * it, 0)
                if not (isinstance(it, int) and it > 0):
                    split_lo(it)
                rows(2 * it + 1, 1)

            steps(dve, NQ // 2, pairs, last=1)
            split_lo(E - 1)

            def add_conv(it, s):
                c = it * RING + s
                dve.wait_ge(conv, c + 1)
                h = Hs[:, :, bass.ds(c * CC, CC)]
                v.tensor_tensor(h, h, bank[6 + s % 2][:, :].rearrange("p (c b) -> p b c", b=B), ALU.add).then_inc(conv_read, 1)

            fence()
            with dve.Fori(0, NCH // RING) as it:
                for s in range(RING):
                    add_conv(it, s)
            fence()

            def row_stats(first, places):
                for b in places:
                    v.bn_stats(stats[:, b, :], Hs[:, bass.ds(first + b, 1), :].rearrange("p b d -> p (b d)"))

            def scales(first, n):
                aggregate(n)
                at_g = bass.ds(first, n)
                rsqrt(n, ln3[:, 0, at_g], EPS_LN)
                v.scalar_tensor_tensor(ln3[:, 1, at_g], mv[:, 0:n, 0], -1.0, ln3[:, 0, at_g], ALU.mult, ALU.mult).then_inc(moments_done, 1)
                fence()

            def choices(i, s):
                dve.wait_ge(logits, i + 1)
                lg = bank[3 + s][:, 0:Q * E].rearrange("p (b e) -> p b e", b=Q)
                for b in range(Q):
                    v.max(top[:, s % 2, b, :], lg[:, b, :])
                fence()
                v.tensor_tensor(wsm[:, 0, bass.ds(i * Q, Q)], top[:, s % 2, :, 1], top[:, s % 2, :, 0], ALU.subtract)
                for b in range(Q):
                    last = v.max_index(topi[:, s * Q + b, :], top[:, s % 2, b, :], lg[:, b, :])
                last.then_inc(gap_ready, 1)

            def group_choices(g):
                fence()
                for k in range(2):
                    v.tensor_copy(e01[:, k, bass.ds(g * GRP, GRP)], topi[:, :, k])

            def shares(g):
                b = bass.ds(g * GRP, GRP)
                dve.wait_ge(exp_done, g + 1)
                v.tensor_scalar(wsm[:, 2, b], wsm[:, 1, b], 1.0, None, ALU.add)
                fence()
                v.reciprocal(wsm[:, 3, b], wsm[:, 2, b])
                fence()
                v.tensor_copy(xrow_f[:, b, D], wsm[:, 3, b])
                v.scalar_tensor_tensor(xrow_f[:, b, D + 1], wsm[:, 1, b], 1.0, wsm[:, 3, b], ALU.subtract, ALU.mult).then_inc(wts_done, 1)

            def hot_experts(g):
                b = bass.ds(g * GRP, GRP)
                for k in range(2):
                    v.tensor_tensor(oh[k][:, :, b], repeat(iota_f[:, 0:E], 2, GRP), repeat(e01[:, k, b], 1, E), ALU.is_equal)

            def hot_sum(g):
                b = bass.ds(g * GRP, GRP)
                v.tensor_tensor(ohb[:, :, b], oh[0][:, :, b], oh[1][:, :, b], ALU.add).then_inc(hot_ready, 1)

            v.memset(onesf, 1.0)
            for first, n in ((0, 2 * Q), (2 * Q, GRP - 2 * Q), (GRP, GRP)):
                row_stats(first, range(n))
                scales(first, n)
            halves = [range(0, GRP // 2), range(GRP // 2, GRP)]

            def groups(g):
                for s in range(QG):
                    i = QG * g + s
                    choices(i, s)
                    if s < 2 and not (isinstance(g, int) and g == 0):
                        (hot_experts, hot_sum)[s](g - 1)
                    if s == QG - 1:
                        group_choices(g)
                    if s == 3 and not (isinstance(g, int) and g == 0):
                        shares(g - 1)
                    if s < 2 and not (isinstance(g, int) and g >= NG - 2):
                        row_stats((g + 2) * GRP, halves[s])
                        if s == 1:
                            scales((g + 2) * GRP, GRP)

            steps(dve, NG, groups, last=2)
            shares(NG - 1)
            fence()

            hot_experts(NG - 1)
            fence()
            hot_sum(NG - 1)

            dve.wait_ge(ranks, NG)
            tot = bank[0][:, :].rearrange("p (e b) -> p e b", e=E)
            for e in range(E):
                v.tensor_tensor_scan(run[:, e, :], onesf, tot[:, e, :], 0.0, ALU.mult, ALU.add)
            fence()
            v.tensor_copy(cnt[:, 0, :], run[:, :, B - 1])
            fence()
            v.tensor_scalar(cnt[:, 0, :], cnt[:, 0, :], float(TS - 1), None, ALU.add)
            fence()
            v.tensor_copy(cnti[:, 0, :], cnt[:, 0, :])
            fence()
            v.tensor_scalar(cnti[:, 1, :], cnti[:, 0, :], 8, None, ALU.logical_shift_right)
            fence()
            v.tensor_copy(cnt[:, 1, :], cnti[:, 1, :])
            fence()
            v.tensor_tensor_scan(cnt[:, 2, :], onesf[:, 0:E], cnt[:, 1, :], 0.0, ALU.mult, ALU.add)
            fence()
            iota_t = bass.AP(tensor=iota_f, offset=0, ap=[[256, 128], [1, NT], [0, E]])
            v.tensor_tensor(eidf, iota_t, repeat(cnt[:, 2, :], 1, NT), ALU.is_ge)
            fence()
            v.tensor_reduce(eidr, eidf, AX.X, ALU.add)
            fence()
            v.tensor_scalar(eid[:, :], eidr[0:1, :], float(E - 1), None, ALU.min).then_inc(eid_done, 1)
            v.tensor_tensor(cnt[:, 3, :], cnt[:, 2, :], cnt[:, 1, :], ALU.subtract)
            v.tensor_tensor(sl, run, tot, ALU.subtract)
            fence()
            v.tensor_tensor(sl, sl, bank[7][:, :].rearrange("p (e b) -> p e b", e=E), ALU.add)
            v.tensor_scalar(cnt[:, 3, :], cnt[:, 3, :], float(TS), None, ALU.mult)
            fence()
            v.tensor_tensor(sl, sl, repeat(cnt[:, 3, :], 2, B), ALU.add)
            fence()
            for k in range(2):
                v.tensor_tensor(oh[k], oh[k], sl, ALU.mult)
            fence()
            for k in range(2):
                v.tensor_reduce(slot[:, :, k], oh[k].rearrange("p e b -> p b e"), AX.X, ALU.add)
            v.tensor_copy(row_v, cst[:, 641 + NC:641 + NC + 2 * B].rearrange("p (b k) -> p b k", k=2))
            fence()
            v.tensor_copy(sloti[:, 0, :, :], slot)
            fence()
            v.tensor_scalar(sloti[:, 1, :, :], sloti[:, 0, :, :], 7, None, ALU.logical_shift_right)
            v.tensor_scalar(sloti[:, 2, :, :], sloti[:, 0, :, :], 127, None, ALU.bitwise_and)
            fence()
            v.tensor_copy(slq, sloti[:, 1, :, :])
            v.tensor_copy(slp, sloti[:, 2, :, :])
            fence()

            dve.wait_ge(w_out, 16 * E)

            def hots(it):
                for a in range(2):
                    n = 2 * it + a
                    b = bass.ds(n * (PICKS // 2), PICKS // 2)

                    def one_hot(out, places, width):
                        return v.tensor_tensor(out, repeat(iota_f[:, 0:width], 1, PICKS),
                                               places[:, b, :].rearrange("p b k -> p (b k)").unsqueeze(2).to_broadcast([128, PICKS, width]),
                                               ALU.is_equal)

                    after(dve, hot_p_ready, n - 1)
                    one_hot(hot_1[:, a, :, :], slp, 128).then_inc(hot_1_ready, 1)
                    after(dve, pick_used, n - 1)
                    one_hot(hot_q[:, a, :, :], slq, NC).then_inc(hot_q_ready, 1)

            steps(dve, B // PICKS, hots)
            dve.wait_ge(table, 1)
            v.tensor_scalar(row_o, bank[6][:, 0:NC], 0.5, None, ALU.is_lt)
            v.tensor_scalar(row_k[:, :], bank[6][:, 0:NC], B * S + 0.5, None, ALU.is_gt)
            v.tensor_scalar(id_f, bank[6][:, 0:NC], 1.0, None, ALU.subtract)
            fence()
            v.scalar_tensor_tensor(id_f, row_k[:, :], -float(B * S), id_f, ALU.mult, ALU.add)
            fence()
            v.tensor_scalar(id_g[:, :], id_f, 0.0, None, ALU.max)
            v.tensor_tensor(row_o, row_o, cst[:, 641:641 + NC], ALU.mult)
            fence()
            v.tensor_tensor(id_s[:, :], id_f, row_o, ALU.add)
            fence()
            dve.sem_inc(ids_done, 1)

            def stage_tile(q, w):
                v.tensor_copy(gi[:, w, :], id_g[:, bass.ds(2 * q, 2)]).then_inc(stage_done, 1)

            def transposed(q, w):
                dve.wait_ge(xg_t, q + 1)
                v.tensor_copy(xgT[:, w, :, :], bank[0][:, :].bitcast(bf16)[:, 0:3 * TS].rearrange("p (c n) -> p c n", c=3)).then_inc(xgT_ready, 1)

            def weights(q, w):
                for h in range(2):
                    v.scalar_tensor_tensor(wk[:, w, h:h + 1], xg_f[:, w, h, D + 1:D + 2], row_k[:, bass.ds(2 * q + h, 1)],
                                           xg_f[:, w, h, D:D + 1], ALU.mult, ALU.add)

            def split_hidden(q, w, blocks):
                for c in blocks:
                    dve.wait_ge(gelu, FC // 2 * q + c // 2 + 1)
                    last = v.tensor_tensor(hl[w][:, c:c + 2, :], hf[w][:, c:c + 2, :], hh[w][:, c:c + 2, :], ALU.subtract)
                return last

            def bias_out(q, w):
                for h in range(2):
                    after(dve, scat[h], 16 * (q - W3 + 1))
                dve.wait_ge(down, q + 1)
                v.tensor_copy(si[:, w, :], id_s[:, bass.ds(2 * q, 2)])
                v.tensor_tensor(yo[:, w, :, :], bank[5 + w][:, 0:2 * D].rearrange("p (h d) -> p h d", h=2),
                                repeat(parts(wbuf[w])[5], 1, 2), ALU.add).then_inc(biased, 1)
                fence()
                for h in range(2):
                    last = v.tensor_scalar(yo[:, w, h, :], yo[:, w, h, :], wk[:, w, h:h + 1], None, ALU.mult)
                last.then_inc(yo_ready, 1)

            dve.wait_ge(h_out, 16 * (NG + 1))
            stage_tile(0, 0)
            stage_tile(1, 1)
            transposed(0, 0)

            def tiles(it):
                for w in range(W3):
                    q = W3 * it + w
                    if isinstance(q, int) and q >= NT:
                        break
                    weights(q, w)
                    if not (isinstance(q, int) and q + 2 >= NT):
                        stage_tile(q + 2, (w + 2) % W3)
                    after(dve, down, q - W3 + 1)
                    split_hidden(q, w, (0, 2))
                    if not (isinstance(q, int) and q + 1 >= NT):
                        transposed(q + 1, (w + 1) % W3)
                    split_hidden(q, w, (4,)).then_inc(hid, 1)
                    if not (isinstance(q, int) and q == 0):
                        bias_out(q - 1, (w - 1) % W3)

            steps(dve, ROUNDS, tiles, last=1)
            bias_out(NT - 1, (NT - 1) % W3)


def kernel(**inputs):
    import numpy as np
    import concourse.bacc as bacc
    from concourse.bass_utils import run_bass_kernel_spmd

    a = {k: np.asarray(x) for k, x in inputs.items()}
    L = "L0_tok_"
    t = np.linspace(0.0, 1.0, S).astype(np.float32)
    w = 2.0 * np.pi * np.linspace(0.0, float(S - 1), S) / S
    zT = np.stack([t, np.cos(1e-4 * w), -np.sin(1e-4 * w)]).astype(np.float32)[:, ::-1]
    r = np.arange(128, dtype=np.float32)
    cst = np.concatenate([np.eye(128, dtype=np.float32), (r[:, None] < r[None, :]).astype(np.float32),
                          np.tile(np.arange(256, dtype=np.float32), (128, 1)), np.tile(t[::-1], (128, 1)), r[:, None],
                          (B * S + 1 + r[:, None] + 128 * (np.arange(NC) % 2)[None, :]).astype(np.float32),
                          (1 + r[:, None, None] + S * np.arange(B)[None, :, None] + B * S * np.arange(2)[None, None, :])
                          .reshape(128, 2 * B).astype(np.float32)], axis=1)
    Wi, Wo = a["L0_ffn_Wi"], a["L0_ffn_Wo"]
    wiT = Wi.transpose(0, 2, 1)
    rest = wiT[:, D0:, :]
    wsrc = np.concatenate([wiT[:, :D0, :], np.concatenate([rest, rest], axis=1),
                           Wo.transpose(0, 2, 1).reshape(E, FC, 128, D).transpose(0, 2, 1, 3).reshape(E, 128, FC * D)], axis=2)
    ids = np.stack([a["x"], a["itok_BS_1_30519"], a["itok_BS_0_30521"], a["itok_BS_1_30520"]])
    col = lambda x: x[:, None]
    arrays = {
        "ids": ids.transpose(2, 0, 1).reshape(S, -1),
        "cst": cst,
        "adj0": a["fside_BSS_adj_cooc"], "adj1": a["fside_BSS_adj_het"], "adj2": a["fside_BSS_adj_isg"],
        "word_emb": a[L + "word_emb"], "pos": a[L + "pos_emb"], "WpT": a[L + "W_proj"].T,
        "b_proj": a[L + "b_proj"], "gamma_beta": np.concatenate([a[L + "ln_gamma"], a[L + "ln_beta"]]),
        "WgT": np.concatenate([a[L + "W_cooc"].T, a[L + "W_het"].T, a[L + "W_isg"].T], axis=1),
        "gbias": col(np.concatenate([a[L + "b_cooc"], a[L + "b_het"], a[L + "b_isg"]])),
        "WrT": a["L0_ffn_Wr"].T,
        "filt": np.stack([a["L0_attn_deltas_abs"], a["L0_attn_b3"], a["L0_attn_bias"]], axis=1),
        "net": np.concatenate([a["L0_attn_w2"].T, a["L0_attn_w3"].T,
                               np.stack([a["L0_attn_b1"], a["L0_attn_b2"], a["L0_attn_freq"]], axis=1)], axis=1),
        "net_in": np.concatenate([a["L0_attn_w1"].T, zT], axis=1),
        "wsrc": wsrc, "bi": a["L0_ffn_bi"].reshape(E, FC, 128).transpose(0, 2, 1), "bo": a["L0_ffn_bo"][:, None, :],
    }
    nc = bacc.Bacc("TRN2", target_bir_lowering=False, num_devices=1)
    feeds, handles = {}, {}
    for name, x in arrays.items():
        feeds[f"in_{name}"] = np.ascontiguousarray(x)
        handles[name] = nc.dram_tensor(f"in_{name}", x.shape, mybir.dt.from_np(x.dtype), kind="ExternalInput").ap()
    handles["adj"] = [handles[f"adj{j}"] for j in range(GRAPHS)]
    out = nc.dram_tensor("out_0", (B * S + SPARE, D), mybir.dt.float32, kind="ExternalOutput").ap()
    tower(nc, handles, out)
    res = run_bass_kernel_spmd(nc, [feeds], core_ids=[0])
    return res.results[0]["out_0"][0:B * S].reshape(B, S, D)
```
